# Optimizing a Trainium2 kernel written in Bass

```python
import numpy as np
import jax
import jax.numpy as jnp

def _softmax(x, axis=-1):
    return jax.nn.softmax(x, axis=axis)

def _gelu(x):
    return jax.nn.gelu(x, approximate=True)

def _silu(x):
    return jax.nn.silu(x)

def _sigmoid(x):
    return jax.nn.sigmoid(x)

def _layernorm(x, axis=-1, eps=1e-05):
    m = jnp.mean(x, axis=axis, keepdims=True)
    v = jnp.var(x, axis=axis, keepdims=True)
    return (x - m) / jnp.sqrt(v + eps)

def _scatter_add(tgt, idx, src, axis=0):
    return tgt.at[idx].add(src)

def _segment_sum(src, seg, n):
    return jax.ops.segment_sum(src, seg, n)
kernel_name = 'mk_adj_resnorm_d2_adj_r2_f9028f'

def setup_inputs(seed: int=0):
    np.random.seed(seed)
    _w = jnp.asarray

    def _rec_inputs():
        import jax
        import jax.numpy as jnp
        _gk = jax.random.key(seed)
        x = -0.0002928 + 1 * jax.random.normal(jax.random.fold_in(_gk, 1), (16, 512, 256), jnp.float32)
        _a = jax.random.bernoulli(jax.random.fold_in(_gk, 2), 0.015625, (16, 512, 512))
        _a = jnp.logical_or(_a, jnp.swapaxes(_a, -1, -2))
        _a = jnp.logical_or(_a, jnp.eye(512, dtype=bool))
        _af = _a.astype(jnp.float32)
        _af = _af * jax.random.uniform(jax.random.fold_in(_gk, 3), (16, 512, 512), jnp.float32, 0.05, 1)
        adj = _af
        return (x, adj)
    x, adj = _rec_inputs()

    def _L0_gnn_setup():
        import jax, jax.numpy as jnp
        import numpy as np
        B, N, DIN, DOUT, K = (4, 1024, 256, 256, 3)
        key = jax.random.key(seed)
        ks = jax.random.split(key, 8)
        X = jax.random.normal(ks[0], (B, N, DIN), dtype=jnp.float32)
        A = jax.random.uniform(ks[1], (B, N, N), dtype=jnp.float32)
        Wv = jax.random.normal(ks[2], (DIN, DOUT), dtype=jnp.float32) * 0.02
        bv = jax.random.normal(ks[3], (DOUT,), dtype=jnp.float32) * 0.02
        aw = jax.random.normal(ks[4], (2 * DOUT, 1), dtype=jnp.float32) * 0.05
        ab = jax.random.normal(ks[5], (1,), dtype=jnp.float32) * 0.05
        Wk = jax.random.normal(ks[6], (K, DIN, DOUT), dtype=jnp.float32) * 0.02
        bk = jax.random.normal(ks[7], (K, DOUT), dtype=jnp.float32) * 0.02
        return {'X': X, 'A': A, 'Wv': Wv, 'bv': bv, 'aw': aw, 'ab': ab, 'Wk': Wk, 'bk': bk}
    _L0_gnn_all = _L0_gnn_setup()
    _L0_gnn_in = {k: v for k, v in _L0_gnn_all.items() if k in ('Wv', 'bv', 'aw', 'ab', 'Wk', 'bk')}
    del _L0_gnn_all

    def _L1_gnn_setup():
        import jax, jax.numpy as jnp
        import numpy as np
        B, N, D = (8, 1024, 256)
        key = jax.random.key(seed)
        ks = jax.random.split(key, 8)
        scale = 0.5 / np.sqrt(D)
        x = jax.random.normal(ks[0], (B, N, D), dtype=jnp.float32)
        adj = jax.random.uniform(ks[1], (B, N, N), dtype=jnp.float32)
        Wq_w = jax.random.normal(ks[2], (D, D), dtype=jnp.float32) * scale
        Wk_w = jax.random.normal(ks[3], (D, D), dtype=jnp.float32) * scale
        Wv_w = jax.random.normal(ks[4], (D, D), dtype=jnp.float32) * scale
        Wq_b = jnp.zeros((D,), dtype=jnp.float32)
        Wk_b = jnp.zeros((D,), dtype=jnp.float32)
        Wv_b = jnp.zeros((D,), dtype=jnp.float32)
        return {'x': x, 'adj': adj, 'Wq_w': Wq_w, 'Wq_b': Wq_b, 'Wk_w': Wk_w, 'Wk_b': Wk_b, 'Wv_w': Wv_w, 'Wv_b': Wv_b}
    _L1_gnn_all = _L1_gnn_setup()
    _L1_gnn_in = {k: v for k, v in _L1_gnn_all.items() if k in ('Wq_w', 'Wq_b', 'Wk_w', 'Wk_b', 'Wv_w', 'Wv_b')}
    del _L1_gnn_all
    return {'x': x, 'adj': adj, 'L0_gnn_Wv': _L0_gnn_in['Wv'], 'L0_gnn_bv': _L0_gnn_in['bv'], 'L0_gnn_aw': _L0_gnn_in['aw'], 'L0_gnn_ab': _L0_gnn_in['ab'], 'L0_gnn_Wk': _L0_gnn_in['Wk'], 'L0_gnn_bk': _L0_gnn_in['bk'], 'L1_gnn_Wq_w': _L1_gnn_in['Wq_w'], 'L1_gnn_Wq_b': _L1_gnn_in['Wq_b'], 'L1_gnn_Wk_w': _L1_gnn_in['Wk_w'], 'L1_gnn_Wk_b': _L1_gnn_in['Wk_b'], 'L1_gnn_Wv_w': _L1_gnn_in['Wv_w'], 'L1_gnn_Wv_b': _L1_gnn_in['Wv_b']}

def reference(x, adj, L0_gnn_Wv, L0_gnn_bv, L0_gnn_aw, L0_gnn_ab, L0_gnn_Wk, L0_gnn_bk, L1_gnn_Wq_w, L1_gnn_Wq_b, L1_gnn_Wk_w, L1_gnn_Wk_b, L1_gnn_Wv_w, L1_gnn_Wv_b):
    import jax
    import jax.numpy as jnp

    def _L0_gnn_ref(X, A, Wv, bv, aw, ab, Wk, bk):
        import jax, jax.numpy as jnp
        import numpy as np
        B, N, DIN, DOUT, K = (4, 1024, 256, 256, 3)
        d = Wv.shape[1]
        Xw = X @ Wv + bv
        sj = Xw @ aw[:d, 0]
        si = Xw @ aw[d:, 0]
        e = jax.nn.leaky_relu(sj[:, None, :] + si[:, :, None] + ab[0], negative_slope=0.2)
        alpha_matrix = A * jnp.exp(e)
        transition = alpha_matrix / (jnp.sum(alpha_matrix, axis=-1, keepdims=True) + 1e-12)
        H = jnp.zeros(X.shape[:-1] + (d,), dtype=X.dtype)
        Xk = X
        for k in range(Wk.shape[0]):
            H = H + Xk @ Wk[k] + bk[k]
            Xk = jnp.einsum('bij,bjd->bid', transition, Xk)
        return jax.nn.relu(H)

    def _L1_gnn_ref(x, adj, Wq_w, Wq_b, Wk_w, Wk_b, Wv_w, Wv_b):
        import jax, jax.numpy as jnp
        import numpy as np
        B, N, D = (8, 1024, 256)
        query = jnp.einsum('bnd,od->bno', x, Wq_w) + Wq_b
        keyt = jnp.einsum('bnd,od->bno', x, Wk_w) + Wk_b
        value = jnp.einsum('bnd,od->bno', x, Wv_w) + Wv_b
        weight = jnp.einsum('bqd,bkd->bqk', query, keyt)
        weight = adj * jnp.exp(weight)
        weight = weight / jnp.sum(weight, axis=2, keepdims=True)
        return jnp.einsum('bqk,bkd->bqd', weight, value)
    x = _layernorm(x + _L0_gnn_ref(x, adj, L0_gnn_Wv, L0_gnn_bv, L0_gnn_aw, L0_gnn_ab, L0_gnn_Wk, L0_gnn_bk), axis=-1)
    x = _layernorm(x + _L1_gnn_ref(x, adj, L1_gnn_Wq_w, L1_gnn_Wq_b, L1_gnn_Wk_w, L1_gnn_Wk_b, L1_gnn_Wv_w, L1_gnn_Wv_b), axis=-1)
    return x

_drawn_inputs = setup_inputs


def setup_inputs(seed=0):
    import zlib

    import numpy as np

    out = dict(_drawn_inputs(seed))
    spreads = {'L1_gnn_Wq_b': (0.0, 0.1), 'L1_gnn_Wk_b': (0.0, 0.8), 'L1_gnn_Wv_b': (0.0, 0.1)}
    factors = {'L0_gnn_Wv': 3.752, 'L0_gnn_bv': 8.0, 'L0_gnn_aw': 3.841}
    for name, (base, spread) in spreads.items():
        noise = np.random.default_rng([zlib.crc32(name.encode()), seed]).standard_normal(out[name].shape)
        drawn = base * np.exp(spread * noise) if base else spread * noise
        out[name] = jnp.asarray(drawn.astype(out[name].dtype))
    for name, factor in factors.items():
        out[name] = (out[name] * factor).astype(out[name].dtype)
    return out
```

```python
import concourse.bass as bass
from concourse import mybir
from contextlib import ExitStack




def gnn_two_layer_kernel(nc, x, x_t, adj_t, w0_all, wv0, bv0, aw, ab, bk0, wq, wk, wv_t,
                         bq_row, bk_row, bq_col, bk_col, bv1, out):
    f32 = mybir.dt.float32
    f32r = mybir.dt.float32r
    ALU = mybir.AluOpType
    ACT = mybir.ActivationFunctionType

    P = 128
    B, N, D = x.shape
    T = N // P
    C = D // P
    E = D + 2
    NEG_SLOPE = 0.2
    EPS = 1e-5
    FIRST_LOOPED, LAST_LOOPED = 2, B - 3
    PAIRS = (LAST_LOOPED - FIRST_LOOPED + 1) // 2
    assert (FIRST_LOOPED, N, D) == (2, 512, 256) and 2 * PAIRS == LAST_LOOPED - 1

    ctx = ExitStack()
    with ctx:
        def sb(name, shape, dt=f32):
            return ctx.enter_context(nc.sbuf_tensor(name, shape, dt))

        def sem(name, n=None):
            if n is None:
                return ctx.enter_context(nc.semaphore(name))
            return [ctx.enter_context(nc.semaphore(f"{name}_{t}")) for t in range(n)]

        ident = sb("ident", [P, P])
        minus_half = sb("minus_half", [P, T])
        one_zero = sb("one_zero", [P, T, 2])
        w_hi = sb("w_hi", [P, C, 2 * D + E], f32r)
        w_lo = sb("w_lo", [P, C, 2 * D + E], f32r)
        m_hi = sb("m_hi", [P, C, D], f32r)
        m_lo = sb("m_lo", [P, C, D], f32r)
        wv_hi = sb("wv_hi", [P, C, E], f32r)
        wv_lo = sb("wv_lo", [P, C, E], f32r)
        u0_bias = sb("u0_bias", [P, E])
        bv1_row = sb("bv1_row", [P, D])
        g_bias = sb("g_bias", [P, C])
        gamma_bias = sb("gamma_bias", [P, 1])

        adj = sb("adj_sb", [P, 2, T, N])
        x_sb = sb("x_sb", [P, 2, T, D])
        xt = sb("xt", [P, 2, C, N])
        xt_hi = sb("xt_hi", [P, C, N], f32r)
        xt_lo = sb("xt_lo", [P, C, N], f32r)
        u0 = sb("u0", [P, 2, T, E])
        xw1 = sb("xw1", [P, T, D])
        y2_hi = sb("y2_hi", [P, T, E], f32r)
        y2_lo = sb("y2_lo", [P, T, D], f32r)
        sj_slope = sb("sj_slope", [P, T])
        e1 = sb("e1", [P, 2, N])
        e2 = sb("e2", [P, 2, N])
        alpha = sb("alpha", [P, 2, N])
        alpha_hi = sb("alpha_hi", [P, 2, T, N], f32r)
        alpha_lo = sb("alpha_lo", [P, 2, T, N], f32r)
        y1 = sb("y1", [P, 2, D])
        y1_hi = sb("y1_hi", [P, T, D], f32r)
        y1_lo = sb("y1_lo", [P, T, D], f32r)
        sum0 = sb("sum0", [P, T])
        inv0 = sb("inv0", [P, T])
        h = sb("h", [P, 2, D])
        x1 = sb("x1", [P, T, D])
        x1_bv = sb("x1_bv", [P, T, D])
        x1t_hi = sb("x1t_hi", [P, C, N], f32r)
        x1t_lo = sb("x1t_lo", [P, C, N], f32r)
        g_hi = sb("g_hi", [P, C, N], f32r)
        g_lo = sb("g_lo", [P, C, N], f32r)
        v_hi = sb("v_hi", [P, T, E], f32r)
        v_lo = sb("v_lo", [P, T, D], f32r)
        gamma = sb("gamma", [P, T])
        p_hi = sb("p_hi", [P, T, N], f32r)
        p_lo = sb("p_lo", [P, T, N], f32r)
        inv1 = sb("inv1", [P, T])
        stats0 = sb("stats0", [P, T, 6])
        stats1 = sb("stats1", [P, T, 6])
        mv0 = sb("mv0", [P, T, 2])
        mv1 = sb("mv1", [P, T, 2])
        var0 = sb("var0", [P, T])
        var1 = sb("var1", [P, T])
        rstd0 = sb("rstd0", [P, T])
        rstd1 = sb("rstd1", [P, T])
        shift0 = sb("shift0", [P, T])
        shift1 = sb("shift1", [P, T])
        shared = sb("shared", [P, 5 * T * D])
        r = shared[:, 0:1024].rearrange("p (t d) -> p t d", t=T)
        r2 = shared[:, 1024:2048].rearrange("p (t d) -> p t d", t=T)
        out_sb = shared[:, 2048:3072].rearrange("p (t d) -> p t d", t=T)
        p_exp = shared[:, 3072:4096].rearrange("p (s n) -> p s n", s=2)
        p_full = shared[:, 4096:5120].rearrange("p (s n) -> p s n", s=2)
        w_raw = shared[:, 0:2 * (2 * D + E)].rearrange("p (c n) -> p c n", c=C)
        at = 2 * (2 * D + E)

        def stage(n):
            nonlocal at
            at += n
            return shared[:, at - n:at]
        wv0_raw = stage(C * D).rearrange("p (c n) -> p c n", c=C)
        wq_raw = stage(C * D).rearrange("p (c n) -> p c n", c=C)
        wk_raw = stage(C * D).rearrange("p (c n) -> p c n", c=C)
        wvt_raw = stage(C * E).rearrange("p (c n) -> p c n", c=C)
        aw_row = stage(2 * D)
        bv0_row = stage(D)
        bq_b = stage(D)
        bk_b = stage(D)
        ab_col = stage(1)
        zc = stage(4)
        bq_c = stage(C)
        bk_c = stage(C)
        assert at <= 5 * T * D
        bk0_rows = alpha_stage = x1_bv[:, :, :].rearrange("p t d -> p (t d)")[:, 0:3 * D]
        scratch = x1[:, :, :].rearrange("p t d -> p (t d)")[:, 0:D]
        m_f = h[:, :, :]

        ps = [ctx.enter_context(nc.psum_tensor(f"bank{i}", [P, N], f32)) for i in range(8)]
        SCORES = [ps[0], ps[1], ps[2], ps[7]]
        TY2 = [ps[3], ps[4], ps[5], ps[7]]
        XW12 = [ps[6], ps[1], ps[2], ps[4]]
        XW0S = [ps[0], ps[7], ps[3], ps[5]]
        SI = ps[7]
        TY1 = [ps[6], ps[0], ps[1], ps[2]]
        PV = [ps[3], ps[4], ps[5], ps[6]]
        X1T = [ps[0], ps[1]]
        G = [ps[2], ps[3]]
        V = [ps[4], ps[5], ps[6], ps[7]]

        w0_loaded, w1_loaded = sem("w0_loaded"), sem("w1_loaded")
        adj_loaded, x_loaded, xt_loaded = sem("adj_loaded", 2), sem("x_loaded", 2), sem("xt_loaded", 2)
        out_stored = sem("out_stored")
        consts_made = sem("consts_made")
        wa_made, w_split, u0_bias_made = sem("wa_made"), sem("w_split"), sem("u0_bias_made")
        m_done, m_split, setup_step = sem("m_done"), sem("m_split"), sem("setup_step")
        ones_made = sem("ones_made")
        w12_done, w0s_done, si_done = sem("w12_done"), sem("w0s_done"), sem("si_done")
        ty2_done, ty1_done, pv_done = sem("ty2_done"), sem("ty1_done"), sem("pv_done")
        scores_done, x1t_done = sem("scores_done"), sem("x1t_done")
        g_done, v_done = sem("g_done"), sem("v_done")
        xw1_ready, y2_hi_ready, y1_hi_ready = sem("xw1_ready"), sem("y2_hi_ready"), sem("y1_hi_ready")
        exps_ready, x1_ready, out_ready = sem("exps_ready"), sem("x1_ready"), sem("out_ready")
        p_exp_ready, p_hi_ready = sem("p_exp_ready"), sem("p_hi_ready")
        x1t_hi_ready, g_hi_ready, v_hi_ready = sem("x1t_hi_ready"), sem("g_hi_ready"), sem("v_hi_ready")
        u0_ready, y2_lo_ready, sj_slope_ready = sem("u0_ready"), sem("y2_lo_ready"), sem("sj_slope_ready")
        sum0_ready, inv0_ready = sem("sum0_ready"), sem("inv0_ready")
        y1_ready, y1_lo_ready = sem("y1_ready"), sem("y1_lo_ready")
        max_ready, alpha_ready = sem("max_ready"), sem("alpha_ready")
        p_ready, p_lo_ready = sem("p_ready"), sem("p_lo_ready")
        h_ready, r_ready, stats0_ready, mv0_ready = sem("h_ready"), sem("r_ready"), sem("stats0_ready"), sem("mv0_ready")
        inv1_ready, r2_ready, stats1_ready, mv1_ready = sem("inv1_ready"), sem("r2_ready"), sem("stats1_ready"), sem("mv1_ready")
        x1t_lo_ready, g_lo_ready, v_lo_ready = sem("x1t_lo_ready"), sem("g_lo_ready"), sem("v_lo_ready")
        gamma_ready = sem("gamma_ready")
        xt_hi_ready, xt_lo_ready = sem("xt_hi_ready"), sem("xt_lo_ready")
        alpha_hi_ready, alpha_lo_ready = sem("alpha_hi_ready"), sem("alpha_lo_ready")
        var0_ready, rstd0_ready, shift0_ready = sem("var0_ready"), sem("rstd0_ready"), sem("shift0_ready")
        var1_ready, rstd1_ready, shift1_ready = sem("var1_ready"), sem("rstd1_ready"), sem("shift1_ready")
        x1_bv_ready = sem("x1_bv_ready")
        passed = sem("passed")

        block = ctx.enter_context(nc.Block())

        class Step:
            def __init__(self, eng, pair, it, values):
                self.eng, self.pair, self.it, self.values = eng, pair, it, values

            def value(self, key, make):
                if key not in self.values:
                    self.values[key] = self.eng.snap(make())
                return self.values[key]

            def tile(self, k, t):
                n = T * (self.it + k) + t + 1
                if self.pair is None:
                    return n
                return self.value(n, lambda: self.pair * (2 * T) + n)

            def chunk(self, k, c):
                return self.tile(k, (c + 1) * (T // 2) - 1)

            def done(self, k):
                return self.tile(k, T - 1)

            def loads(self, k):
                n = 16 * ((self.it + k) // 2 + 1)
                if self.pair is None:
                    return n
                return self.value(("loads", n), lambda: self.pair * 16 + n)

            def stores(self, k):
                n = 16 * (self.it + k + 1)
                if self.pair is None:
                    return n
                return self.value(("stores", n), lambda: self.pair * 32 + n)

            def live(self, k):
                return self.pair is not None or 0 <= self.it + k < B

            def slot(self, k):
                return (self.it + k) % 2

            def graph(self, k):
                return self.it + k if self.pair is None else self.pair * 2 + (self.it + k)

        def steps(eng, step, first):
            for it in range(first, FIRST_LOOPED):
                step(Step(eng, None, it, {}))
            with eng.Fori(1, PAIRS + 1) as pair:
                values = {}
                step(Step(eng, pair, 0, values))
                step(Step(eng, pair, 1, values))
            for it in range(LAST_LOOPED + 1, B):
                step(Step(eng, None, it, {}))

        def wait(eng, semaphore, count):
            if not isinstance(count, int) or count > 0:
                eng.wait_ge(semaphore, count)

        def plain(ap):
            return ap.bitcast(f32)

        @block.sync
        def _(sp):
            def load(dst, src, semaphore):
                sp.dma_start(dst, src).then_inc(semaphore, 16)

            def load_xt(slot, graph):
                load(xt[:, slot, :, :], x_t[graph].rearrange("(p c) n -> p c n", c=C), xt_loaded[slot])

            def load_x(slot, graph):
                load(x_sb[:, slot, :, :], x[graph].rearrange("(p t) d -> p t d", t=T), x_loaded[slot])

            def load_adj(slot, graph):
                load(adj[:, slot, :, :], adj_t[graph].rearrange("(p t) n -> p t n", t=T), adj_loaded[slot])

            load_xt(0, 0)
            load(w_raw[:, :, 0:D], w0_all[1].rearrange("(p c) n -> p c n", c=C), w0_loaded)
            load(w_raw[:, :, D:2 * D], w0_all[2].rearrange("(p c) n -> p c n", c=C), w0_loaded)
            load(w_raw[:, :, 2 * D:3 * D], w0_all[0].rearrange("(p c) n -> p c n", c=C), w0_loaded)
            load(wv0_raw, wv0.rearrange("(p c) n -> p c n", c=C), w0_loaded)
            load(aw_row, aw.to_broadcast([P, 2 * D]), w0_loaded)
            load(bv0_row, bv0.to_broadcast([P, D]), w0_loaded)
            load(ab_col, ab.to_broadcast([P, 1]), w0_loaded)
            load(bk0_rows, bk0.to_broadcast([P, 3 * D]), w0_loaded)
            load_adj(0, 0)
            load_xt(1, 1)
            load(wq_raw, wq.rearrange("(c p) n -> p c n", p=P), w1_loaded)
            load(wk_raw, wk.rearrange("(c p) n -> p c n", p=P), w1_loaded)
            load(wvt_raw[:, :, 0:D], wv_t.rearrange("(c p) n -> p c n", p=P), w1_loaded)
            load(bq_c, bq_col, w1_loaded)
            load(bk_c, bk_col, w1_loaded)
            load(bq_b, bq_row.to_broadcast([P, D]), w1_loaded)
            load(bk_b, bk_row.to_broadcast([P, D]), w1_loaded)
            load(bv1_row[:, :], bv1.to_broadcast([P, D]), w1_loaded)
            load_x(0, 0)
            load_adj(1, 1)
            load_x(1, 1)

            def step(at):
                if at.live(0) and at.live(2):
                    wait(sp, xt_lo_ready, at.done(0))
                    load_xt(at.slot(2), at.graph(2))
                    wait(sp, r_ready, at.tile(0, T - 1))
                    load_x(at.slot(2), at.graph(2))
                if at.live(-1):
                    wait(sp, out_ready, at.done(-1))
                    sp.dma_start(out[at.graph(-1)].rearrange("(p t) d -> p t d", t=T),
                                 out_sb).then_inc(out_stored, 16)
                if at.live(0) and at.live(2):
                    wait(sp, p_ready, at.tile(0, T - 1))
                    load_adj(at.slot(2), at.graph(2))

            steps(sp, step, 0)
            sp.wait_ge(out_ready, T * B)
            sp.dma_start(out[B - 1].rearrange("(p t) d -> p t d", t=T), out_sb).then_inc(out_stored, 16)
            sp.wait_ge(out_stored, 16 * B)

        @block.tensor
        def _(pe):
            def product(dst, terms):
                for n, (stationary, moving) in enumerate(terms):
                    width = moving.shape[-1]
                    last = pe.matmul(dst[:, 0:width], stationary, moving,
                                     start=(n == 0), stop=(n == len(terms) - 1))
                return last

            def nodes(t):
                return slice(t * P, (t + 1) * P)

            def scores(at):
                wait(pe, g_lo_ready, at.done(0))
                for t in range(T):
                    if t == T - 1:
                        wait(pe, v_lo_ready, at.done(0))
                    product(SCORES[t], [
                        (s[:, c, nodes(t)], m[:, c, :])
                        for c in range(C) for s, m in ((g_hi, x1t_hi), (g_hi, x1t_lo), (g_lo, x1t_hi))
                    ]).then_inc(scores_done, 1)

            def transition(at, dst, hi, lo, done, k):
                a_hi, a_lo = alpha_hi[:, at.slot(k), :, :], alpha_lo[:, at.slot(k), :, :]
                return product(dst, [
                    term for j in range(T) for term in (
                        (a_hi[:, j, done], hi[:, j, :]), (a_lo[:, j, done], hi[:, j, :]), (a_hi[:, j, done], lo[:, j, :]))
                ])

            def ty2(at):
                wait(pe, alpha_lo_ready, at.done(1))
                wait(pe, y2_lo_ready, at.done(1))
                for t in range(T):
                    if t == T - 1:
                        wait(pe, p_exp_ready, at.done(0))
                    transition(at, TY2[t], y2_hi, y2_lo, nodes(t), 1).then_inc(ty2_done, 1)

            def xw(at):
                wait(pe, xt_lo_ready, at.done(2))
                for t in range(T):
                    if t == 1:
                        wait(pe, y1_ready, at.done(1))
                    n = 0
                    for c in range(C):
                        for xs, ws in ((xt_hi, (w_hi, w_lo)), (xt_lo, (w_hi,))):
                            for w in ws:
                                n += 1
                                for dst, done, lo, hi in ((XW12, w12_done, 0, 2 * D), (XW0S, w0s_done, 2 * D, 2 * D + E)):
                                    last = pe.matmul(dst[t][:, 0:hi - lo], xs[:, c, nodes(t)], w[:, c, lo:hi],
                                                     start=(n == 1), stop=(n == 3 * C))
                                    if n == 3 * C:
                                        last.then_inc(done, 1)

            def si_rows(at):
                wait(pe, u0_ready, at.done(2))
                for t in range(T):
                    column = u0[:, at.slot(2), t, D + 1:D + 2]
                    last = pe.transpose(SI[:, nodes(t)], column.to_broadcast([P, P]), ident[:, :])
                last.then_inc(si_done, T)

            def ty1(at, t):
                if t == 0:
                    wait(pe, y1_lo_ready, at.done(1))
                    if at.live(2):
                        wait(pe, y2_lo_ready, at.tile(2, 0))
                transition(at, TY1[t], y1_hi, y1_lo, nodes(t), 1).then_inc(ty1_done, 1)

            def pv(at, t):
                if t == 0:
                    wait(pe, p_lo_ready, at.done(0))
                elif t == 1 and at.live(2):
                    wait(pe, y2_lo_ready, at.done(2))
                elif t == 3 and at.live(1):
                    wait(pe, h_ready, at.tile(1, 0))
                product(PV[t], [
                    term for j in range(T) for term in (
                        (p_hi[:, j, nodes(t)], v_hi[:, j, :]), (p_lo[:, j, nodes(t)], v_hi[:, j, :]),
                        (p_hi[:, j, nodes(t)], v_lo[:, j, :]))
                ]).then_inc(pv_done, 1)

            def x1_transposes(at):
                wait(pe, x1_ready, at.done(1))
                for c in range(C):
                    for t in range(T):
                        last = pe.transpose(X1T[c][:, nodes(t)], x1[:, t, nodes(c)], ident[:, :])
                    last.then_inc(x1t_done, 2)

            def g_product(at):
                wait(pe, x1t_lo_ready, at.done(1))
                for c in range(C):
                    if c == 1 and at.live(0):
                        wait(pe, r2_ready, at.tile(0, 0))
                    product(G[c], [
                        (s[:, cc, nodes(c)], m[:, cc, :])
                        for cc in range(C) for s, m in ((m_hi, x1t_hi), (m_hi, x1t_lo), (m_lo, x1t_hi))
                    ]).then_inc(g_done, 2)

            def v_product(at):
                for t in range(T):
                    if t < T - 1:
                        if at.live(0):
                            wait(pe, r2_ready, at.tile(0, t + 1))
                        elif t == 0:
                            wait(pe, y2_lo_ready, at.done(2))
                    elif at.live(2):
                        wait(pe, exps_ready, at.tile(2, T - 1))
                    product(V[t], [
                        (s[:, c, nodes(t)], m[:, c, :])
                        for c in range(C) for s, m in ((x1t_hi, wv_hi), (x1t_hi, wv_lo), (x1t_lo, wv_hi))
                    ]).then_inc(v_done, 1)

            def step(at):
                if at.it == -1 and at.pair is None:
                    pe.wait_ge(m_split, 1)
                if at.live(0):
                    scores(at)
                if at.live(1):
                    ty2(at)
                if at.live(2):
                    xw(at)
                if at.live(1):
                    ty1(at, 0)
                if at.live(2):
                    si_rows(at)
                if at.live(1):
                    for t in range(1, T):
                        ty1(at, t)
                if at.live(0):
                    for t in range(T - 1):
                        pv(at, t)
                if at.live(1):
                    x1_transposes(at)
                if at.live(0):
                    pv(at, T - 1)
                if at.live(1):
                    g_product(at)
                    v_product(at)
                if at.it == -2 and at.pair is None:
                    pe.wait_ge(w1_loaded, 16 * 8)
                    pe.wait_ge(u0_ready, T)
                    pe.wait_ge(y2_lo_ready, T)
                    for c in range(C):
                        product(ps[c], [(wk_raw[:, o, nodes(c)], wq_raw[:, o, :]) for o in range(C)])
                        product(ps[2][:, c:c + 1], [(wq_raw[:, o, nodes(c)], bk_c[:, o:o + 1]) for o in range(C)])
                        last = product(ps[3][:, c:c + 1], [(wk_raw[:, o, nodes(c)], bq_c[:, o:o + 1]) for o in range(C)])
                    last.then_inc(m_done, 1)

            pe.wait_ge(w_split, 2)
            pe.wait_ge(consts_made, 4)
            steps(pe, step, -2)

        @block.scalar
        def _(act):
            def step(at):
                s0, s1, s2 = at.slot(0), at.slot(1), at.slot(2)

                def exp_p(t):
                    wait(act, scores_done, at.tile(0, t))
                    wait(act, gamma_ready, at.tile(0, t))
                    if t >= 2:
                        wait(act, p_ready, at.tile(0, t - 2))
                    else:
                        wait(act, p_ready, at.tile(-1, t + 2))
                    act.activation(p_exp[:, t % 2, :], SCORES[t][:, :], ACT.Exp,
                                   bias=gamma[:, t:t + 1]).then_inc(p_exp_ready, 1)

                def hi_p(t):
                    wait(act, p_ready, at.tile(0, t))
                    if t == 0:
                        wait(act, pv_done, at.done(-1))
                    act.activation(p_hi[:, t, :], p_full[:, t % 2, :], ACT.Copy).then_inc(p_hi_ready, 1)

                if at.live(0):
                    exp_p(0)
                    exp_p(1)
                    hi_p(0)
                    exp_p(2)
                    hi_p(1)
                    exp_p(3)
                    hi_p(2)
                    hi_p(3)
                if at.live(1):
                    for t in range(T):
                        wait(act, y1_ready, at.tile(1, t))
                        if t == 0:
                            wait(act, ty1_done, at.done(0))
                        act.activation(y1_hi[:, t, :], y1[:, t % 2, :], ACT.Copy).then_inc(y1_hi_ready, 1)
                if at.live(2):
                    for t in range(T):
                        wait(act, w12_done, at.tile(2, t))
                        if t == 0:
                            wait(act, y1_ready, at.done(1))
                        act.activation(xw1[:, t, :], XW12[t][:, 0:D], ACT.Copy).then_inc(xw1_ready, 1)
                        act.activation(y2_hi[:, t, 0:D], XW12[t][:, D:2 * D], ACT.Copy).then_inc(y2_hi_ready, 1)

                def exps(t):
                    if t == 0:
                        wait(act, si_done, at.done(2))
                        wait(act, sj_slope_ready, at.done(2))
                    if t >= 2:
                        wait(act, alpha_ready, at.tile(2, t - 2))
                    else:
                        wait(act, alpha_ready, at.tile(1, t + 2))
                    act.activation(e1[:, t % 2, :], SI[:, :], ACT.Exp, bias=u0[:, s2, t, D:D + 1])
                    act.activation(e2[:, t % 2, :], SI[:, :], ACT.Exp, scale=NEG_SLOPE,
                                   bias=sj_slope[:, t:t + 1]).then_inc(exps_ready, 1)

                def norm0(t):
                    if t == 0:
                        wait(act, x1_bv_ready, at.done(0))
                        wait(act, x1t_done, at.done(0))
                    if t % 2 == 0:
                        wait(act, shift0_ready, at.chunk(1, t // 2))
                    act.activation(x1[:, t, :], r[:, t, :], ACT.Identity, scale=rstd0[:, t:t + 1],
                                   bias=shift0[:, t:t + 1]).then_inc(x1_ready, 1)

                if at.live(2):
                    exps(0)
                    exps(1)
                if at.live(1):
                    norm0(0)
                    norm0(1)
                    norm0(2)
                    norm0(3)
                if at.live(2):
                    exps(2)
                    exps(3)
                if at.live(1):
                    for c in range(C):
                        wait(act, x1t_done, at.chunk(1, c))
                        if c == 0:
                            wait(act, scores_done, at.done(0))
                        act.activation(x1t_hi[:, c, :], X1T[c][:, :], ACT.Copy).then_inc(x1t_hi_ready, 2)
                    for c in range(C):
                        wait(act, g_done, at.chunk(1, c))
                        act.activation(g_hi[:, c, :], G[c][:, :], ACT.Identity,
                                       bias=g_bias[:, c:c + 1]).then_inc(g_hi_ready, 2)
                    for t in range(T):
                        wait(act, v_done, at.tile(1, t))
                        if t == 0:
                            wait(act, pv_done, at.done(0))
                        act.activation(v_hi[:, t, 0:D], V[t][:, 0:D], ACT.Copy).then_inc(v_hi_ready, 1)
                if at.live(0):
                    for t in range(T):
                        if t == 0:
                            wait(act, out_stored, at.stores(-1))
                        if t % 2 == 0:
                            wait(act, shift1_ready, at.chunk(0, t // 2))
                        norm = act.activation(out_sb[:, t, :], r2[:, t, :], ACT.Identity,
                                              scale=rstd1[:, t:t + 1], bias=shift1[:, t:t + 1])
                    norm.then_inc(out_ready, T)

            act.wait_ge(ones_made, 2)
            steps(act, step, -2)

        @block.vector
        def _(dve):
            def split_lo(dst, src, hi):
                return dve.tensor_tensor(dst, src, plain(hi), ALU.subtract)

            def dot(n, semaphore, dst, a, b):
                dve.wait_ge(setup_step, n)
                dve.scalar_tensor_tensor(scratch, a, 1.0, b, ALU.mult, ALU.mult, accum_out=dst).then_inc(semaphore, 1)

            dve.wait_ge(w0_loaded, 16 * 8)
            for c in range(C):
                for half in range(2):
                    n = 2 * c + half
                    dot(n, setup_step, w_raw[:, c, 3 * D + half:3 * D + half + 1], wv0_raw[:, c, :],
                        aw_row[:, half * D:(half + 1) * D])
            n = 2 * C
            dot(n, setup_step, zc[:, 0:1], bv0_row, aw_row[:, 0:D])
            dot(n + 1, setup_step, zc[:, 1:2], bv0_row, aw_row[:, D:2 * D])
            dve.wait_ge(setup_step, n + 2)
            dve.tensor_copy(w_hi[:, :, :], w_raw).then_inc(w_split, 1)
            dve.wait_ge(w_split, 1)
            split_lo(w_lo[:, :, :], w_raw, w_hi[:, :, :]).then_inc(w_split, 1)
            dve.tensor_tensor(zc[:, 2:3], zc[:, 0:1], zc[:, 1:2], ALU.add).then_inc(setup_step, 1)
            dve.memset(u0_bias[:, D:E], 0.0).then_inc(setup_step, 1)
            dve.tensor_tensor(u0_bias[:, 0:D], bk0_rows[:, 0:D], bk0_rows[:, D:2 * D], ALU.add).then_inc(setup_step, 1)
            dve.wait_ge(setup_step, n + 5)
            dve.tensor_tensor(u0_bias[:, D:D + 1], zc[:, 2:3], ab_col, ALU.add).then_inc(setup_step, 1)
            dve.tensor_tensor(u0_bias[:, 0:D], u0_bias[:, 0:D], bk0_rows[:, 2 * D:3 * D], ALU.add).then_inc(setup_step, 1)
            dve.wait_ge(setup_step, n + 7)
            dve.wait_ge(consts_made, 4)
            dve.tensor_copy(y2_hi[:, :, D:E], one_zero[:, :, :]).then_inc(ones_made, 1)
            dve.tensor_copy(v_hi[:, :, D:E], one_zero[:, :, :]).then_inc(ones_made, 1)

            def xw_steps(at):
                for t in range(T):
                    wait(dve, w0s_done, at.tile(2, t))
                    dve.tensor_tensor(u0[:, at.slot(2), t, :], XW0S[t][:, 0:E], u0_bias[:, :], ALU.add).then_inc(u0_ready, 1)
                    wait(dve, y2_hi_ready, at.tile(2, t))
                    split_lo(y2_lo[:, t, :], XW12[t][:, D:2 * D], y2_hi[:, t, 0:D]).then_inc(y2_lo_ready, 1)
                wait(dve, u0_ready, at.tile(2, T - 1))
                wait(dve, exps_ready, at.tile(1, T - 1))
                dve.tensor_scalar(sj_slope[:, :], u0[:, at.slot(2), :, D:D + 1].rearrange("p t o -> p (t o)"),
                                  NEG_SLOPE, None, ALU.mult).then_inc(sj_slope_ready, T)

            def step(at):
                s0, s1, s2 = at.slot(0), at.slot(1), at.slot(2)

                def p_mul(t):
                    wait(dve, p_exp_ready, at.tile(0, t))
                    other, k = (t - 2, 0) if t >= 2 else (t + 2, -1)
                    wait(dve, p_lo_ready, at.tile(k, other))
                    dve.tensor_tensor(p_full[:, t % 2, :], p_exp[:, t % 2, :], adj[:, s0, t, :],
                                      ALU.mult).then_inc(p_ready, 1)

                def p_split(t):
                    wait(dve, p_hi_ready, at.tile(0, t))
                    split_lo(p_lo[:, t, :], p_full[:, t % 2, :], p_hi[:, t, :]).then_inc(p_lo_ready, 1)

                if at.live(0):
                    p_mul(0)
                    p_mul(1)
                    p_split(0)
                    p_mul(2)
                    p_split(1)
                    p_mul(3)
                    p_split(2)
                    p_split(3)

                def y1_sum(t):
                    wait(dve, ty2_done, at.tile(1, t))
                    dve.tensor_scalar(sum0[:, t:t + 1], TY2[t][:, D:D + 1], 1e-12, None, ALU.add).then_inc(sum0_ready, 1)

                def y1_inv(t):
                    wait(dve, sum0_ready, at.tile(1, t))
                    dve.reciprocal(inv0[:, t:t + 1], sum0[:, t:t + 1]).then_inc(inv0_ready, 1)

                def y1_full(t):
                    wait(dve, inv0_ready, at.tile(1, t))
                    wait(dve, xw1_ready, at.tile(1, t))
                    other, k = (t - 2, 1) if t >= 2 else (t + 2, 0)
                    wait(dve, y1_lo_ready, at.tile(k, other))
                    dve.scalar_tensor_tensor(y1[:, t % 2, :], TY2[t][:, 0:D], inv0[:, t:t + 1], xw1[:, t, :],
                                             ALU.mult, ALU.add).then_inc(y1_ready, 1)

                def y1_split(t):
                    wait(dve, y1_hi_ready, at.tile(1, t))
                    split_lo(y1_lo[:, t, :], y1[:, t % 2, :], y1_hi[:, t, :]).then_inc(y1_lo_ready, 1)

                if at.live(1):
                    for t in range(T):
                        y1_sum(t)
                        y1_inv(t)
                        y1_full(t)
                        if t:
                            y1_split(t - 1)
                    y1_split(T - 1)
                if at.live(2):
                    xw_steps(at)

                def a_max(t):
                    if at.live(2):
                        wait(dve, exps_ready, at.tile(2, t))
                        dve.tensor_tensor(e1[:, t % 2, :], e1[:, t % 2, :], e2[:, t % 2, :], ALU.max).then_inc(max_ready, 1)

                def a_mul(t):
                    if at.live(2):
                        wait(dve, max_ready, at.tile(2, t))
                        if t == 0:
                            wait(dve, adj_loaded[s2], at.loads(2))
                        other, k = (t - 2, 2) if t >= 2 else (t + 2, 1)
                        wait(dve, alpha_lo_ready, at.tile(k, other))
                        dve.tensor_tensor(alpha[:, t % 2, :], e1[:, t % 2, :], adj[:, s2, t, :],
                                          ALU.mult).then_inc(alpha_ready, 1)

                def h_sum(t):
                    if at.live(1):
                        wait(dve, ty1_done, at.tile(1, t))
                        other, k = (t - 2, 1) if t >= 2 else (t + 2, 0)
                        wait(dve, r_ready, at.tile(k, other))
                        dve.scalar_tensor_tensor(h[:, t % 2, :], TY1[t][:, 0:D], inv0[:, t:t + 1], u0[:, s1, t, 0:D],
                                                 ALU.mult, ALU.add).then_inc(h_ready, 1)

                def residual0(t):
                    if at.live(1):
                        wait(dve, h_ready, at.tile(1, t))
                        if t == 0:
                            wait(dve, x_loaded[s1], at.loads(1))
                        wait(dve, x1_ready, at.tile(0, t))
                        dve.scalar_tensor_tensor(r[:, t, :], h[:, t % 2, :], 0.0, x_sb[:, s1, t, :],
                                                 ALU.max, ALU.add).then_inc(r_ready, 1)

                def stat0(t):
                    if at.live(1):
                        wait(dve, r_ready, at.tile(1, t))
                        dve.bn_stats(stats0[:, t, :], r[:, t, :]).then_inc(stats0_ready, 1)

                def mean_var0(t):
                    if at.live(1):
                        wait(dve, stats0_ready, at.tile(1, t))
                        wait(dve, shift0_ready, at.chunk(0, t // 2))
                        dve.sem_inc(passed, 1)
                        dve.bn_aggr(mv0[:, t, :], stats0[:, t, :]).then_inc(mv0_ready, 1)

                def inverse1(t):
                    if at.live(0):
                        wait(dve, pv_done, at.tile(0, t))
                        dve.reciprocal(inv1[:, t:t + 1], PV[t][:, D:D + 1]).then_inc(inv1_ready, 1)

                def residual1(t):
                    if at.live(0):
                        wait(dve, inv1_ready, at.tile(0, t))
                        wait(dve, x1_bv_ready, at.tile(0, t))
                        wait(dve, out_ready, at.done(-1))
                        dve.scalar_tensor_tensor(r2[:, t, :], PV[t][:, 0:D], inv1[:, t:t + 1], x1_bv[:, t, :],
                                                 ALU.mult, ALU.add).then_inc(r2_ready, 1)

                def stat1(t):
                    if at.live(0):
                        wait(dve, r2_ready, at.tile(0, t))
                        dve.bn_stats(stats1[:, t, :], r2[:, t, :]).then_inc(stats1_ready, 1)

                def mean_var1(t):
                    if at.live(0):
                        wait(dve, stats1_ready, at.tile(0, t))
                        wait(dve, shift1_ready, at.chunk(-1, t // 2))
                        dve.sem_inc(passed, 1)
                        dve.bn_aggr(mv1[:, t, :], stats1[:, t, :]).then_inc(mv1_ready, 1)

                h_sum(0)
                a_max(0)
                residual0(0)
                h_sum(1)
                stat0(0)
                residual0(1)
                mean_var0(0)
                h_sum(2)
                stat0(1)
                residual0(2)
                mean_var0(1)
                h_sum(3)
                stat0(2)
                residual0(3)
                mean_var0(2)
                a_mul(0)
                stat0(3)
                a_max(1)
                mean_var0(3)
                inverse1(0)
                a_mul(1)
                residual1(0)
                a_max(2)
                inverse1(1)
                stat1(0)
                residual1(1)
                a_mul(2)
                mean_var1(0)
                inverse1(2)
                stat1(1)
                residual1(2)
                mean_var1(1)
                if at.live(1):
                    for c in range(C):
                        wait(dve, x1t_hi_ready, at.chunk(1, c))
                        split_lo(x1t_lo[:, c, :], X1T[c][:, :], x1t_hi[:, c, :]).then_inc(x1t_lo_ready, 2)
                inverse1(3)
                stat1(2)
                residual1(3)
                mean_var1(2)
                a_max(3)
                stat1(3)
                a_mul(3)
                mean_var1(3)
                if at.live(1):
                    for c in range(C):
                        wait(dve, g_hi_ready, at.chunk(1, c))
                        dve.scalar_tensor_tensor(g_lo[:, c, :], G[c][:, :], g_bias[:, c:c + 1], plain(g_hi[:, c, :]),
                                                 ALU.add, ALU.subtract).then_inc(g_lo_ready, 2)
                    for t in range(T):
                        wait(dve, v_hi_ready, at.tile(1, t))
                        dve.tensor_tensor(gamma[:, t:t + 1], V[t][:, D:D + 1], gamma_bias[:, :], ALU.add).then_inc(gamma_ready, 1)
                        split_lo(v_lo[:, t, :], V[t][:, 0:D], v_hi[:, t, 0:D]).then_inc(v_lo_ready, 1)

                if at.it == -2 and at.pair is None:
                    dve.wait_ge(m_done, 1)
                    dve.tensor_copy(g_bias[:, :], ps[2][:, 0:C]).then_inc(setup_step, 1)
                    for c in range(C):
                        dve.tensor_copy(wvt_raw[:, c, D:D + 1], ps[3][:, c:c + 1]).then_inc(setup_step, 1)
                        dve.memset(wvt_raw[:, c, D + 1:E], 0.0).then_inc(setup_step, 1)
                        dve.tensor_copy(m_hi[:, c, :], ps[c][:, 0:D]).then_inc(setup_step, 1)
                    dve.wait_ge(setup_step, 2 * C + 7 + 1 + 3 * C)
                    dve.tensor_copy(wv_hi[:, :, :], wvt_raw).then_inc(setup_step, 1)
                    dve.scalar_tensor_tensor(scratch, bq_b, 1.0, bk_b, ALU.mult, ALU.mult,
                                             accum_out=gamma_bias[:, :]).then_inc(setup_step, 1)
                    for c in range(C):
                        split_lo(m_lo[:, c, :], ps[c][:, 0:D], m_hi[:, c, :]).then_inc(setup_step, 1)
                    dve.wait_ge(setup_step, 2 * C + 7 + 1 + 3 * C + 2 + C)
                    split_lo(wv_lo[:, :, :], wvt_raw, wv_hi[:, :, :]).then_inc(m_split, 1)
                    dve.wait_ge(m_split, 1)

            steps(dve, step, -2)

        @block.gpsimd
        def _(pool):
            def hi(dst, src):
                return pool.tensor_scalar(dst, src, 1.0, 0.0, ALU.mult, ALU.add)

            pool.memset(ident[:, :], 0.0).then_inc(consts_made, 1)
            pool.memset(minus_half[:, :], -0.5).then_inc(consts_made, 1)
            pool.memset(one_zero[:, :, 0:1], 1.0)
            pool.memset(one_zero[:, :, 1:2], 0.0).then_inc(consts_made, 1)
            pool.wait_ge(consts_made, 3)
            pool.affine_select(out=ident[:, :], in_=ident[:, :], compare_op=ALU.not_equal, fill=1.0, base=0,
                               pattern=[[-1, P]], channel_multiplier=1).then_inc(consts_made, 1)

            def layernorm_scale(at, k, pair, mv, mv_ready, var, var_ready, rstd, rstd_ready, shift, shift_ready, read, tile):
                a, b = 2 * pair, 2 * pair + 2
                wait(pool, mv_ready, at.tile(k, b - 1))
                wait(pool, read, at.tile(k - 1, tile))
                pool.sem_inc(passed, 1)
                pool.tensor_scalar(var[:, a:b], mv[:, a:b, 1:2].rearrange("p t o -> p (t o)"), EPS, None,
                                   ALU.add).then_inc(var_ready, 2)
                wait(pool, var_ready, at.chunk(k, pair))
                pool.tensor_tensor(rstd[:, a:b], var[:, a:b], minus_half[:, a:b], ALU.pow).then_inc(rstd_ready, 2)
                wait(pool, rstd_ready, at.chunk(k, pair))
                pool.sem_inc(passed, 1)
                for t in range(a, b):
                    last = pool.tensor_scalar(shift[:, t:t + 1], mv[:, t, 0:1], rstd[:, t:t + 1], -1.0,
                                              ALU.mult, ALU.mult)
                last.then_inc(shift_ready, 2)

            def alpha_split(at, t):
                other = alpha[:, t % 2, :]
                wait(pool, alpha_ready, at.tile(2, t))
                wait(pool, ty1_done, at.tile(0, T - 1))
                pool.sem_inc(passed, 1)
                hi(alpha_hi[:, at.slot(2), t, :], other).then_inc(alpha_hi_ready, 1)
                wait(pool, alpha_hi_ready, at.tile(2, t))
                pool.tensor_tensor(alpha_lo[:, at.slot(2), t, :], other, plain(alpha_hi[:, at.slot(2), t, :]),
                                   ALU.subtract).then_inc(alpha_lo_ready, 1)

            def step(at):
                if at.live(2):
                    for c in range(C):
                        if c == 0:
                            wait(pool, xt_loaded[at.slot(2)], at.loads(2))
                            wait(pool, w0s_done, at.tile(1, T - 1))
                            pool.sem_inc(passed, 1)
                        split = hi(xt_hi[:, c, :], xt[:, at.slot(2), c, :])
                    split.then_inc(xt_hi_ready, T)
                    wait(pool, xt_hi_ready, at.done(2))
                    for c in range(C):
                        split = pool.tensor_tensor(xt_lo[:, c, :], xt[:, at.slot(2), c, :], plain(xt_hi[:, c, :]), ALU.subtract)
                    split.then_inc(xt_lo_ready, T)
                if at.live(1):
                    layernorm_scale(at, 1, 0, mv0, mv0_ready, var0, var0_ready, rstd0, rstd0_ready, shift0, shift0_ready, x1_ready, 1)
                if at.live(1):
                    layernorm_scale(at, 1, 1, mv0, mv0_ready, var0, var0_ready, rstd0, rstd0_ready, shift0, shift0_ready, x1_ready, 3)
                if at.live(2):
                    alpha_split(at, 0)
                    alpha_split(at, 1)
                if at.live(0):
                    layernorm_scale(at, 0, 0, mv1, mv1_ready, var1, var1_ready, rstd1, rstd1_ready, shift1, shift1_ready, out_ready, T - 1)
                if at.live(2):
                    alpha_split(at, 2)
                if at.live(0):
                    layernorm_scale(at, 0, 1, mv1, mv1_ready, var1, var1_ready, rstd1, rstd1_ready, shift1, shift1_ready, out_ready, T - 1)
                if at.live(1):
                    for t in range(T):
                        wait(pool, x1_ready, at.tile(1, t))
                        wait(pool, r2_ready, at.tile(0, t))
                        if at.it == -1 and at.pair is None:
                            pool.wait_ge(w1_loaded, 16 * 8)
                            pool.wait_ge(m_split, 1)
                        pool.tensor_tensor(x1_bv[:, t, :], x1[:, t, :], bv1_row[:, :], ALU.add).then_inc(x1_bv_ready, 1)
                if at.live(2):
                    alpha_split(at, 3)

            steps(pool, step, -2)


def kernel(**inputs):
    import numpy as _np
    import concourse.bacc as _bacc
    from concourse import mybir as _mybir
    from concourse.bass_utils import run_bass_kernel_spmd as _run

    a = {k: _np.asarray(v) for k, v in inputs.items()}
    x, adj = a["x"], a["adj"]
    B, N, D = x.shape
    x_t = x.reshape(B, 128, N // 128, D).transpose(0, 3, 2, 1).reshape(B, D, N)
    adj_t = adj.reshape(B, 128, N // 128, N).transpose(0, 3, 2, 1).reshape(B, N, N)
    arrays = {
        "x": x, "x_t": x_t, "adj_t": adj_t,
        "w0_all": a["L0_gnn_Wk"], "wv0": a["L0_gnn_Wv"],
        "bv0": a["L0_gnn_bv"].reshape(1, -1), "aw": a["L0_gnn_aw"].reshape(1, -1),
        "ab": a["L0_gnn_ab"].reshape(1, 1), "bk0": a["L0_gnn_bk"].reshape(1, -1),
        "wq": a["L1_gnn_Wq_w"], "wk": a["L1_gnn_Wk_w"], "wv_t": a["L1_gnn_Wv_w"].T,
        "bq_row": a["L1_gnn_Wq_b"].reshape(1, -1), "bk_row": a["L1_gnn_Wk_b"].reshape(1, -1),
        "bq_col": a["L1_gnn_Wq_b"].reshape(-1, 128).T, "bk_col": a["L1_gnn_Wk_b"].reshape(-1, 128).T,
        "bv1": a["L1_gnn_Wv_b"].reshape(1, -1),
    }
    arrays = {f"in_{k}_dram": _np.ascontiguousarray(v) for k, v in arrays.items()}
    nc = _bacc.Bacc("TRN2", target_bir_lowering=False, num_devices=1)
    args = [nc.dram_tensor(k, v.shape, _mybir.dt.from_np(v.dtype), kind="ExternalInput").ap() for k, v in arrays.items()]
    args.append(nc.dram_tensor("out_dram", (B, N, D), _mybir.dt.float32, kind="ExternalOutput").ap())
    gnn_two_layer_kernel(nc, *args)
    r = _run(nc, [arrays], core_ids=[0])
    return r.results[0]["out_dram"]
```

```python
import concourse.bass as bass
from concourse import mybir
from contextlib import ExitStack




def gnn_two_layer_kernel(nc, x, x_t, adj_t, w0_all, wv0, bv0, aw, ab, bk0, wq, wk, wv_t,
                         bq_row, bk_row, bq_col, bk_col, bv1, out):
    f32 = mybir.dt.float32
    f32r = mybir.dt.float32r
    ALU = mybir.AluOpType
    ACT = mybir.ActivationFunctionType

    P = 128
    B, N, D = x.shape
    T = N // P
    C = D // P
    E = D + 2
    NEG_SLOPE = 0.2
    EPS = 1e-5
    FIRST_LOOPED, LAST_LOOPED = 2, B - 3
    PAIRS = (LAST_LOOPED - FIRST_LOOPED + 1) // 2
    assert (FIRST_LOOPED, N, D) == (2, 512, 256) and 2 * PAIRS == LAST_LOOPED - 1

    ctx = ExitStack()
    with ctx:
        def sb(name, shape, dt=f32):
            return ctx.enter_context(nc.sbuf_tensor(name, shape, dt))

        def sem(name, n=None):
            if n is None:
                return ctx.enter_context(nc.semaphore(name))
            return [ctx.enter_context(nc.semaphore(f"{name}_{t}")) for t in range(n)]

        ident = sb("ident", [P, P])
        minus_half = sb("minus_half", [P, T])
        one_zero = sb("one_zero", [P, T, 2])
        w_hi = sb("w_hi", [P, C, 2 * D + E], f32r)
        w_lo = sb("w_lo", [P, C, 2 * D + E], f32r)
        m_hi = sb("m_hi", [P, C, D], f32r)
        m_lo = sb("m_lo", [P, C, D], f32r)
        wv_hi = sb("wv_hi", [P, C, E], f32r)
        wv_lo = sb("wv_lo", [P, C, E], f32r)
        u0_bias = sb("u0_bias", [P, E])
        bv1_row = sb("bv1_row", [P, D])
        g_bias = sb("g_bias", [P, C])
        gamma_bias = sb("gamma_bias", [P, 1])

        adj = sb("adj_sb", [P, 2, T, N])
        x_sb = sb("x_sb", [P, 2, T, D])
        xt = sb("xt", [P, 2, C, N])
        xt_hi = sb("xt_hi", [P, C, N], f32r)
        xt_lo = sb("xt_lo", [P, C, N], f32r)
        u0 = sb("u0", [P, 2, T, E])
        xw1 = sb("xw1", [P, T, D])
        y2_hi = sb("y2_hi", [P, T, E], f32r)
        y2_lo = sb("y2_lo", [P, T, D], f32r)
        sj_slope = sb("sj_slope", [P, T])
        alpha = sb("alpha", [P, T, N])
        e2 = sb("e2", [P, 2, N])
        alpha_hi = sb("alpha_hi", [P, 2, T, N], f32r)
        alpha_lo = sb("alpha_lo", [P, 2, T, N], f32r)
        y1 = sb("y1", [P, 2, D])
        y1_hi = sb("y1_hi", [P, T, D], f32r)
        y1_lo = sb("y1_lo", [P, T, D], f32r)
        sum0 = sb("sum0", [P, T])
        inv0 = sb("inv0", [P, T])
        h = sb("h", [P, 2, D])
        x1 = sb("x1", [P, T, D])
        x1_bv = sb("x1_bv", [P, T, D])
        x1t_hi = sb("x1t_hi", [P, C, N], f32r)
        x1t_lo = sb("x1t_lo", [P, C, N], f32r)
        g_hi = sb("g_hi", [P, C, N], f32r)
        g_lo = sb("g_lo", [P, C, N], f32r)
        v_hi = sb("v_hi", [P, T, E], f32r)
        v_lo = sb("v_lo", [P, T, D], f32r)
        gamma = sb("gamma", [P, T])
        p_hi = sb("p_hi", [P, T, N], f32r)
        p_lo = sb("p_lo", [P, T, N], f32r)
        inv1 = sb("inv1", [P, T])
        stats0 = sb("stats0", [P, T, 6])
        stats1 = sb("stats1", [P, T, 6])
        mv0 = sb("mv0", [P, T, 2])
        mv1 = sb("mv1", [P, T, 2])
        var0 = sb("var0", [P, T])
        var1 = sb("var1", [P, T])
        rstd0 = sb("rstd0", [P, T])
        rstd1 = sb("rstd1", [P, T])
        shift1 = sb("shift1", [P, T])
        shared = sb("shared", [P, 5 * T * D])
        r = shared[:, 0:1024].rearrange("p (t d) -> p t d", t=T)
        r2 = shared[:, 1024:2048].rearrange("p (t d) -> p t d", t=T)
        out_sb = shared[:, 2048:3072].rearrange("p (t d) -> p t d", t=T)
        p_full = shared[:, 3072:5120].rearrange("p (t n) -> p t n", t=T)
        w_raw = shared[:, 0:2 * (2 * D + E)].rearrange("p (c n) -> p c n", c=C)
        at = 2 * (2 * D + E)

        def stage(n):
            nonlocal at
            at += n
            return shared[:, at - n:at]
        wv0_raw = stage(C * D).rearrange("p (c n) -> p c n", c=C)
        wq_raw = stage(C * D).rearrange("p (c n) -> p c n", c=C)
        wk_raw = stage(C * D).rearrange("p (c n) -> p c n", c=C)
        wvt_raw = stage(C * E).rearrange("p (c n) -> p c n", c=C)
        aw_row = stage(2 * D)
        bv0_row = stage(D)
        bq_b = stage(D)
        bk_b = stage(D)
        ab_col = stage(1)
        zc = stage(4)
        bq_c = stage(C)
        bk_c = stage(C)
        assert at <= 5 * T * D
        bk0_rows = x1_bv[:, :, :].rearrange("p t d -> p (t d)")[:, 0:3 * D]
        dots = p_hi[:, :, :].rearrange("p t n -> p (t n)").rearrange("p (s d) -> p s d", d=D)

        ps = [ctx.enter_context(nc.psum_tensor(f"bank{i}", [P, N], f32)) for i in range(8)]
        SCORES = [ps[0], ps[1], ps[2], ps[7]]
        TY2 = [ps[3], ps[4], ps[5], ps[7]]
        XW12 = [ps[6], ps[1], ps[3], ps[4]]
        XW0S = [ps[0], ps[2], ps[7], ps[5]]
        SI = ps[7]
        TY1 = [ps[6], ps[0], ps[1], ps[2]]
        PV = [ps[3], ps[6], ps[4], ps[5]]
        X1T = [ps[0], ps[1]]
        G = [ps[2], ps[3]]
        V = [ps[6], ps[4], ps[5], ps[7]]

        w12_loaded, w0_loaded, wa_loaded = sem("w12_loaded"), sem("w0_loaded"), sem("wa_loaded")
        wqk_loaded, w1_loaded = sem("wqk_loaded"), sem("w1_loaded")
        adj_loaded, x_loaded, xt_loaded = sem("adj_loaded", 2), sem("x_loaded", 2), sem("xt_loaded", 2)
        out_stored = sem("out_stored")
        consts_made = sem("consts_made")
        w12_split, w0s_split = sem("w12_split"), sem("w0s_split")
        m_done, m_split, setup_step = sem("m_done"), sem("m_split"), sem("setup_step")
        ones_made = sem("ones_made")
        w12_done, w0s_done, si_done = sem("w12_done"), sem("w0s_done"), sem("si_done")
        ty2_done, ty1_done, pv_done = sem("ty2_done"), sem("ty1_done"), sem("pv_done")
        scores_done, x1t_done = sem("scores_done"), sem("x1t_done")
        g_done, v_done = sem("g_done"), sem("v_done")
        xw1_ready, y2_hi_ready, y1_hi_ready = sem("xw1_ready"), sem("y2_hi_ready"), sem("y1_hi_ready")
        exps_ready, x1_ready, out_ready = sem("exps_ready"), sem("x1_ready"), sem("out_ready")
        p_exp_ready, p_hi_ready = sem("p_exp_ready"), sem("p_hi_ready")
        x1t_hi_ready, g_hi_ready, v_hi_ready = sem("x1t_hi_ready"), sem("g_hi_ready"), sem("v_hi_ready")
        u0_ready, y2_lo_ready, sj_slope_ready = sem("u0_ready"), sem("y2_lo_ready"), sem("sj_slope_ready")
        sum0_ready, inv0_ready = sem("sum0_ready"), sem("inv0_ready")
        y1_ready, y1_lo_ready = sem("y1_ready"), sem("y1_lo_ready")
        max_ready, alpha_ready = sem("max_ready"), sem("alpha_ready")
        p_ready, p_lo_ready = sem("p_ready"), sem("p_lo_ready")
        h_ready, r_ready, stats0_ready, mv0_ready = sem("h_ready"), sem("r_ready"), sem("stats0_ready"), sem("mv0_ready")
        inv1_ready, r2_ready, stats1_ready, mv1_ready = sem("inv1_ready"), sem("r2_ready"), sem("stats1_ready"), sem("mv1_ready")
        x1t_lo_ready, g_lo_ready, v_lo_ready = sem("x1t_lo_ready"), sem("g_lo_ready"), sem("v_lo_ready")
        gamma_ready = sem("gamma_ready")
        xt_hi_ready, xt_lo_ready = sem("xt_hi_ready"), sem("xt_lo_ready")
        alpha_hi_ready, alpha_lo_ready = sem("alpha_hi_ready"), sem("alpha_lo_ready")
        var0_ready, rstd0_ready = sem("var0_ready"), sem("rstd0_ready")
        var1_ready, rstd1_ready, shift1_ready = sem("var1_ready"), sem("rstd1_ready"), sem("shift1_ready")
        x1_bv_ready = sem("x1_bv_ready")
        passed = sem("passed")

        block = ctx.enter_context(nc.Block())

        class Step:
            def __init__(self, eng, pair, it, values):
                self.eng, self.pair, self.it, self.values = eng, pair, it, values

            def value(self, key, make):
                if key not in self.values:
                    self.values[key] = self.eng.snap(make())
                return self.values[key]

            def tile(self, k, t):
                n = T * (self.it + k) + t + 1
                if self.pair is None:
                    return n
                return self.value(n, lambda: self.pair * (2 * T) + n)

            def chunk(self, k, c):
                return self.tile(k, (c + 1) * (T // 2) - 1)

            def done(self, k):
                return self.tile(k, T - 1)

            def loads(self, k):
                n = 16 * ((self.it + k) // 2 + 1)
                if self.pair is None:
                    return n
                return self.value(("loads", n), lambda: self.pair * 16 + n)

            def stores(self, k):
                n = 16 * (self.it + k + 1)
                if self.pair is None:
                    return n
                return self.value(("stores", n), lambda: self.pair * 32 + n)

            def live(self, k):
                return self.pair is not None or 0 <= self.it + k < B

            def slot(self, k):
                return (self.it + k) % 2

            def graph(self, k):
                return self.it + k if self.pair is None else self.pair * 2 + (self.it + k)

        def steps(eng, step, first):
            for it in range(first, FIRST_LOOPED):
                step(Step(eng, None, it, {}))
            with eng.Fori(1, PAIRS + 1) as pair:
                values = {}
                step(Step(eng, pair, 0, values))
                step(Step(eng, pair, 1, values))
            for it in range(LAST_LOOPED + 1, B + 1):
                step(Step(eng, None, it, {}))

        def wait(eng, semaphore, count):
            if not isinstance(count, int) or count > 0:
                eng.wait_ge(semaphore, count)

        def plain(ap):
            return ap.bitcast(f32)

        @block.sync
        def _(sp):
            def load(dst, src, semaphore):
                sp.dma_start(dst, src).then_inc(semaphore, 16)

            def load_xt(slot, graph):
                load(xt[:, slot, :, :], x_t[graph].rearrange("(p c) n -> p c n", c=C), xt_loaded[slot])

            def load_x(slot, graph):
                load(x_sb[:, slot, :, :], x[graph].rearrange("(p t) d -> p t d", t=T), x_loaded[slot])

            def load_adj(slot, graph):
                load(adj[:, slot, :, :], adj_t[graph].rearrange("(p t) n -> p t n", t=T), adj_loaded[slot])

            load_xt(0, 0)
            load(w_raw[:, :, 0:D], w0_all[1].rearrange("(p c) n -> p c n", c=C), w12_loaded)
            load(w_raw[:, :, D:2 * D], w0_all[2].rearrange("(p c) n -> p c n", c=C), w12_loaded)
            load(wv0_raw, wv0.rearrange("(p c) n -> p c n", c=C), wa_loaded)
            load(aw_row, aw.to_broadcast([P, 2 * D]), wa_loaded)
            load(bv0_row, bv0.to_broadcast([P, D]), wa_loaded)
            load(ab_col, ab.to_broadcast([P, 1]), wa_loaded)
            load(w_raw[:, :, 2 * D:3 * D], w0_all[0].rearrange("(p c) n -> p c n", c=C), w0_loaded)
            load(bk0_rows, bk0.to_broadcast([P, 3 * D]), w0_loaded)
            load_xt(1, 1)
            load(wq_raw, wq.rearrange("(c p) n -> p c n", p=P), wqk_loaded)
            load(wk_raw, wk.rearrange("(c p) n -> p c n", p=P), wqk_loaded)
            load(bq_c, bq_col, wqk_loaded)
            load(bk_c, bk_col, wqk_loaded)
            load_adj(0, 0)
            load(wvt_raw[:, :, 0:D], wv_t.rearrange("(c p) n -> p c n", p=P), w1_loaded)
            load(bq_b, bq_row.to_broadcast([P, D]), w1_loaded)
            load(bk_b, bk_row.to_broadcast([P, D]), w1_loaded)
            load(bv1_row[:, :], bv1.to_broadcast([P, D]), w1_loaded)
            load_x(0, 0)
            load_adj(1, 1)
            load_x(1, 1)

            def step(at):
                if at.live(0) and at.live(2):
                    wait(sp, xt_lo_ready, at.done(0))
                    load_xt(at.slot(2), at.graph(2))
                    wait(sp, r_ready, at.tile(0, T - 1))
                    load_x(at.slot(2), at.graph(2))
                if at.live(-1):
                    wait(sp, out_ready, at.done(-1))
                    sp.dma_start(out[at.graph(-1)].rearrange("(p t) d -> p t d", t=T),
                                 out_sb).then_inc(out_stored, 16)
                if at.live(0) and at.live(2):
                    wait(sp, p_ready, at.tile(0, T - 1))
                    load_adj(at.slot(2), at.graph(2))

            steps(sp, step, 0)
            sp.wait_ge(out_stored, 16 * B)

        @block.tensor
        def _(pe):
            def product(dst, terms):
                for n, (stationary, moving) in enumerate(terms):
                    width = moving.shape[-1]
                    last = pe.matmul(dst[:, 0:width], stationary, moving,
                                     start=(n == 0), stop=(n == len(terms) - 1))
                return last

            def nodes(t):
                return slice(t * P, (t + 1) * P)

            def scores(at):
                wait(pe, g_lo_ready, at.done(0))
                for t in range(T):
                    if t == T - 1:
                        wait(pe, v_lo_ready, at.done(0))
                    product(SCORES[t], [
                        (s[:, c, nodes(t)], m[:, c, :])
                        for c in range(C) for s, m in ((g_hi, x1t_hi), (g_hi, x1t_lo), (g_lo, x1t_hi))
                    ]).then_inc(scores_done, 1)

            def transition(at, dst, hi, lo, done, k):
                a_hi, a_lo = alpha_hi[:, at.slot(k), :, :], alpha_lo[:, at.slot(k), :, :]
                return product(dst, [
                    term for j in range(T) for term in (
                        (a_hi[:, j, done], hi[:, j, :]), (a_lo[:, j, done], hi[:, j, :]), (a_hi[:, j, done], lo[:, j, :]))
                ])

            def ty2(at):
                wait(pe, alpha_lo_ready, at.done(1))
                wait(pe, y2_lo_ready, at.done(1))
                for t in range(T):
                    if t == T - 1:
                        wait(pe, p_exp_ready, at.done(0))
                    transition(at, TY2[t], y2_hi, y2_lo, nodes(t), 1).then_inc(ty2_done, 1)

            def xw(at, tiles, parts=("w12", "w0s")):
                if 0 in tiles:
                    wait(pe, xt_lo_ready, at.done(2))
                for t in tiles:
                    if t == 2:
                        wait(pe, y1_ready, at.done(1))
                    passes = [(s[:, c, nodes(t)], w, c) for c in range(C)
                              for s, w in ((xt_hi, w_hi), (xt_hi, w_lo), (xt_lo, w_hi))]
                    for n, (x_part, w_part, c) in enumerate(passes):
                        start, stop = n == 0, n == len(passes) - 1
                        if "w12" in parts:
                            last12 = pe.matmul(XW12[t][:, :], x_part, w_part[:, c, 0:2 * D], start=start, stop=stop)
                        if "w0s" in parts:
                            last0s = pe.matmul(XW0S[t][:, 0:E], x_part, w_part[:, c, 2 * D:2 * D + E], start=start, stop=stop)
                    if "w12" in parts:
                        last12.then_inc(w12_done, 1)
                    if "w0s" in parts:
                        last0s.then_inc(w0s_done, 1)

            def si_rows(at):
                wait(pe, u0_ready, at.done(2))
                for t in range(T):
                    column = u0[:, at.slot(2), t, D + 1:D + 2]
                    last = pe.transpose(SI[:, nodes(t)], column.to_broadcast([P, P]), ident[:, :])
                last.then_inc(si_done, T)

            def ty1(at, t):
                if t == 0:
                    wait(pe, y1_lo_ready, at.done(1))
                if t in (0, 2) and at.live(2):
                    wait(pe, y2_lo_ready, at.tile(2, t // 2))
                transition(at, TY1[t], y1_hi, y1_lo, nodes(t), 1).then_inc(ty1_done, 1)

            def pv(at, t):
                if t == 0:
                    wait(pe, p_lo_ready, at.done(0))
                    if at.live(2):
                        wait(pe, y2_lo_ready, at.tile(2, 2))
                elif t == 1 and at.live(1):
                    wait(pe, h_ready, at.tile(1, 0))
                elif t == 2 and at.live(2):
                    wait(pe, y2_lo_ready, at.done(2))
                product(PV[t], [
                    term for j in range(T) for term in (
                        (p_hi[:, j, nodes(t)], v_hi[:, j, :]), (p_lo[:, j, nodes(t)], v_hi[:, j, :]),
                        (p_hi[:, j, nodes(t)], v_lo[:, j, :]))
                ]).then_inc(pv_done, 1)

            def x1_transposes(at):
                wait(pe, x1_ready, at.done(1))
                for c in range(C):
                    for t in range(T):
                        last = pe.transpose(X1T[c][:, nodes(t)], x1[:, t, nodes(c)], ident[:, :])
                    last.then_inc(x1t_done, T // C)

            def g_product(at):
                for cc in range(C):
                    wait(pe, x1t_lo_ready, at.chunk(1, cc))
                    for c in range(C):
                        if cc == 0 and c == 1 and at.live(0):
                            wait(pe, r2_ready, at.tile(0, 0))
                        terms = ((m_hi, x1t_hi), (m_hi, x1t_lo), (m_lo, x1t_hi))
                        for n, (s, m) in enumerate(terms):
                            last = pe.matmul(G[c][:, :], s[:, cc, nodes(c)], m[:, cc, :],
                                             start=(cc == 0 and n == 0), stop=(cc == C - 1 and n == 2))
                        if cc == C - 1:
                            last.then_inc(g_done, T // C)

            def v_product(at):
                for t in range(T):
                    if t < T - 1:
                        if at.live(0):
                            wait(pe, r2_ready, at.tile(0, t + 1))
                        elif t == 1:
                            wait(pe, y2_lo_ready, at.done(2))
                    elif at.live(2):
                        wait(pe, exps_ready, at.tile(2, T - 1))
                    product(V[t], [
                        (s[:, c, nodes(t)], m[:, c, :])
                        for c in range(C) for s, m in ((x1t_hi, wv_hi), (x1t_hi, wv_lo), (x1t_lo, wv_hi))
                    ]).then_inc(v_done, 1)

            def step(at):
                if at.it == -2 and at.pair is None:
                    first_step(at)
                    return
                ahead = at.it == -1 and at.pair is None
                if at.live(0):
                    scores(at)
                if ahead:
                    pe.wait_ge(m_split, 1)
                    xw(at, (0, 1))
                if at.live(1):
                    ty2(at)
                if at.live(2):
                    xw(at, (2,) if ahead else (0, 1, 2))
                if at.live(1):
                    for t in range(T):
                        ty1(at, t)
                if at.live(2):
                    xw(at, (3,))
                if at.live(0):
                    pv(at, 0)
                if at.live(2):
                    si_rows(at)
                if at.live(0):
                    pv(at, 1)
                if at.live(1):
                    x1_transposes(at)
                if at.live(0):
                    pv(at, 2)
                    pv(at, 3)
                if at.live(1):
                    g_product(at)
                    v_product(at)

            def first_step(at):
                pe.wait_ge(w12_split, 2)
                xw(at, range(T), ("w12",))
                pe.wait_ge(w0s_split, 2)
                xw(at, range(T), ("w0s",))
                pe.wait_ge(consts_made, 4)
                si_rows(at)
                pe.wait_ge(wqk_loaded, 16 * 4)
                pe.wait_ge(y2_lo_ready, T)
                for c in range(C):
                    product(ps[c], [(wk_raw[:, o, nodes(c)], wq_raw[:, o, :]) for o in range(C)])
                    product(ps[2][:, c:c + 1], [(wq_raw[:, o, nodes(c)], bk_c[:, o:o + 1]) for o in range(C)])
                    last = product(ps[2][:, C + c:C + c + 1],
                                   [(wk_raw[:, o, nodes(c)], bq_c[:, o:o + 1]) for o in range(C)])
                last.then_inc(m_done, 1)

            steps(pe, step, -2)

        @block.scalar
        def _(act):
            def step(at):
                s0, s1, s2 = at.slot(0), at.slot(1), at.slot(2)

                def exp_p(t):
                    wait(act, scores_done, at.tile(0, t))
                    wait(act, gamma_ready, at.tile(0, t))
                    wait(act, p_lo_ready, at.tile(-1, t))
                    act.activation(p_full[:, t, :], SCORES[t][:, :], ACT.Exp,
                                   bias=gamma[:, t:t + 1]).then_inc(p_exp_ready, 1)

                def hi_p(t):
                    wait(act, p_ready, at.tile(0, t))
                    if t == 0:
                        wait(act, pv_done, at.done(-1))
                    act.activation(p_hi[:, t, :], p_full[:, t, :], ACT.Copy).then_inc(p_hi_ready, 1)

                if at.live(0):
                    exp_p(0)
                    exp_p(1)
                    hi_p(0)
                    exp_p(2)
                    hi_p(1)
                    exp_p(3)
                    hi_p(2)
                    hi_p(3)
                if at.live(1):
                    for t in range(T):
                        wait(act, y1_ready, at.tile(1, t))
                        if t == 0:
                            wait(act, ty1_done, at.done(0))
                        act.activation(y1_hi[:, t, :], y1[:, t % 2, :], ACT.Copy).then_inc(y1_hi_ready, 1)
                def xw_tile(t):
                    wait(act, w12_done, at.tile(2, t))
                    if t == 0:
                        wait(act, y1_ready, at.done(1))
                    act.activation(xw1[:, t, :], XW12[t][:, 0:D], ACT.Copy).then_inc(xw1_ready, 1)
                    act.activation(y2_hi[:, t, 0:D], XW12[t][:, D:2 * D], ACT.Copy).then_inc(y2_hi_ready, 1)

                if at.live(2):
                    xw_tile(0)
                    xw_tile(1)
                    xw_tile(2)
                if at.live(-1):
                    for t in range(T):
                        if t == 0:
                            wait(act, out_stored, at.stores(-2))
                        if t % 2 == 0:
                            wait(act, shift1_ready, at.chunk(-1, t // 2))
                        norm = act.activation(out_sb[:, t, :], r2[:, t, :], ACT.Identity,
                                              scale=rstd1[:, t:t + 1], bias=shift1[:, t:t + 1])
                    norm.then_inc(out_ready, T)
                if at.live(2):
                    xw_tile(3)

                def exps(t):
                    if at.live(2):
                        if t == 0:
                            wait(act, si_done, at.done(2))
                            wait(act, sj_slope_ready, at.done(2))
                        wait(act, alpha_lo_ready, at.tile(1, t))
                        act.activation(alpha[:, t, :], SI[:, :], ACT.Exp, bias=u0[:, s2, t, D:D + 1])
                        if t < 2:
                            wait(act, max_ready, at.tile(1, t + 2))
                        else:
                            wait(act, max_ready, at.tile(2, t - 2))
                        act.activation(e2[:, t % 2, :], SI[:, :], ACT.Exp, scale=NEG_SLOPE,
                                       bias=sj_slope[:, t:t + 1]).then_inc(exps_ready, 1)

                if at.live(0):
                    exps(0)
                if at.live(1):
                    for c in range(C):
                        wait(act, x1t_done, at.chunk(1, c))
                        if c == 0:
                            wait(act, scores_done, at.done(0))
                        act.activation(x1t_hi[:, c, :], X1T[c][:, :], ACT.Copy).then_inc(x1t_hi_ready, T // C)
                if not at.live(0):
                    exps(0)
                exps(1)
                exps(2)
                exps(3)
                if at.live(1):
                    for c in range(C):
                        wait(act, g_done, at.chunk(1, c))
                        act.activation(g_hi[:, c, :], G[c][:, :], ACT.Identity,
                                       bias=g_bias[:, c:c + 1]).then_inc(g_hi_ready, T // C)
                    for t in range(T):
                        wait(act, v_done, at.tile(1, t))
                        if t == 0:
                            wait(act, pv_done, at.done(0))
                        act.activation(v_hi[:, t, 0:D], V[t][:, 0:D], ACT.Copy).then_inc(v_hi_ready, 1)

            act.wait_ge(ones_made, 2)
            steps(act, step, -2)

        @block.vector
        def _(dve):
            def split_lo(dst, src, hi):
                return dve.tensor_tensor(dst, src, plain(hi), ALU.subtract)

            dve.wait_ge(xt_loaded[0], 16)
            dve.tensor_copy(xt_hi[:, :, :], xt[:, 0, :, :]).then_inc(xt_hi_ready, T)
            dve.wait_ge(xt_hi_ready, T)
            split_lo(xt_lo[:, :, :], xt[:, 0, :, :], xt_hi[:, :, :]).then_inc(xt_lo_ready, T)
            dve.wait_ge(w12_loaded, 16 * 2)
            w12, w0s = slice(0, 2 * D), slice(2 * D, 2 * D + E)
            dve.tensor_copy(w_hi[:, :, w12], w_raw[:, :, w12]).then_inc(w12_split, 1)
            dve.wait_ge(w12_split, 1)
            split_lo(w_lo[:, :, w12], w_raw[:, :, w12], w_hi[:, :, w12]).then_inc(w12_split, 1)
            dve.wait_ge(wa_loaded, 16 * 4)
            wanted = [(w_raw[:, c, 3 * D + half:3 * D + half + 1], wv0_raw[:, c, :], half) for c in range(C) for half in range(2)]
            wanted += [(zc[:, half:half + 1], bv0_row, half) for half in range(2)]
            for n, (dst, row, half) in enumerate(wanted):
                dve.scalar_tensor_tensor(dots[:, n, :], row, 1.0, aw_row[:, half * D:(half + 1) * D],
                                         ALU.mult, ALU.mult, accum_out=dst).then_inc(setup_step, 1)
            dve.wait_ge(w0_loaded, 16 * 2)
            dve.wait_ge(setup_step, len(wanted))
            dve.tensor_copy(w_hi[:, :, w0s], w_raw[:, :, w0s]).then_inc(w0s_split, 1)
            dve.tensor_tensor(u0_bias[:, 0:D], bk0_rows[:, 0:D], bk0_rows[:, D:2 * D], ALU.add).then_inc(setup_step, 1)
            dve.wait_ge(w0s_split, 1)
            split_lo(w_lo[:, :, w0s], w_raw[:, :, w0s], w_hi[:, :, w0s]).then_inc(w0s_split, 1)
            dve.memset(u0_bias[:, D:E], 0.0).then_inc(setup_step, 1)
            dve.tensor_tensor(zc[:, 2:3], zc[:, 0:1], zc[:, 1:2], ALU.add).then_inc(setup_step, 1)
            dve.wait_ge(setup_step, len(wanted) + 3)
            dve.tensor_tensor(u0_bias[:, D:D + 1], zc[:, 2:3], ab_col, ALU.add).then_inc(setup_step, 1)
            dve.tensor_tensor(u0_bias[:, 0:D], u0_bias[:, 0:D], bk0_rows[:, 2 * D:3 * D], ALU.add).then_inc(setup_step, 1)
            layer0_steps = len(wanted) + 5
            dve.wait_ge(setup_step, layer0_steps)
            dve.wait_ge(consts_made, 4)
            dve.tensor_copy(y2_hi[:, :, D:E], one_zero[:, :, :]).then_inc(ones_made, 1)
            dve.tensor_copy(v_hi[:, :, D:E], one_zero[:, :, :]).then_inc(ones_made, 1)

            def xw_steps(at, tiles):
                for t in tiles:
                    wait(dve, w0s_done, at.tile(2, t))
                    dve.tensor_tensor(u0[:, at.slot(2), t, :], XW0S[t][:, 0:E], u0_bias[:, :], ALU.add).then_inc(u0_ready, 1)
                    wait(dve, y2_hi_ready, at.tile(2, t))
                    split_lo(y2_lo[:, t, :], XW12[t][:, D:2 * D], y2_hi[:, t, 0:D]).then_inc(y2_lo_ready, 1)
                if T - 1 in tiles:
                    wait(dve, u0_ready, at.done(2))
                    wait(dve, exps_ready, at.done(1))
                    dve.tensor_scalar(sj_slope[:, :], u0[:, at.slot(2), :, D:D + 1].rearrange("p t o -> p (t o)"),
                                      NEG_SLOPE, None, ALU.mult).then_inc(sj_slope_ready, T)

            def step(at):
                s0, s1, s2 = at.slot(0), at.slot(1), at.slot(2)

                def p_mul(t):
                    if at.live(0):
                        wait(dve, p_exp_ready, at.tile(0, t))
                        dve.tensor_tensor(p_full[:, t, :], p_full[:, t, :], adj[:, s0, t, :],
                                          ALU.mult).then_inc(p_ready, 1)

                def p_split(t):
                    if at.live(0):
                        wait(dve, p_hi_ready, at.tile(0, t))
                        split_lo(p_lo[:, t, :], p_full[:, t, :], p_hi[:, t, :]).then_inc(p_lo_ready, 1)

                def y1_sum(t):
                    wait(dve, ty2_done, at.tile(1, t))
                    dve.tensor_scalar(sum0[:, t:t + 1], TY2[t][:, D:D + 1], 1e-12, None, ALU.add).then_inc(sum0_ready, 1)

                def y1_inv(t):
                    wait(dve, sum0_ready, at.tile(1, t))
                    dve.reciprocal(inv0[:, t:t + 1], sum0[:, t:t + 1]).then_inc(inv0_ready, 1)

                def y1_full(t):
                    wait(dve, inv0_ready, at.tile(1, t))
                    wait(dve, xw1_ready, at.tile(1, t))
                    other, k = (t - 2, 1) if t >= 2 else (t + 2, 0)
                    wait(dve, y1_lo_ready, at.tile(k, other))
                    dve.scalar_tensor_tensor(y1[:, t % 2, :], TY2[t][:, 0:D], inv0[:, t:t + 1], xw1[:, t, :],
                                             ALU.mult, ALU.add).then_inc(y1_ready, 1)

                def y1_split(t):
                    wait(dve, y1_hi_ready, at.tile(1, t))
                    split_lo(y1_lo[:, t, :], y1[:, t % 2, :], y1_hi[:, t, :]).then_inc(y1_lo_ready, 1)

                def y1_tile(t):
                    if at.live(1):
                        y1_sum(t)
                        y1_inv(t)
                        y1_full(t)

                p_mul(0)
                p_mul(1)
                p_split(0)
                p_mul(2)
                p_split(1)
                p_mul(3)
                p_split(2)
                y1_tile(0)
                p_split(3)
                y1_tile(1)
                if at.live(1):
                    y1_split(0)
                y1_tile(2)
                if at.live(1):
                    y1_split(1)
                y1_tile(3)
                if at.live(1):
                    y1_split(2)
                    y1_split(3)
                if at.live(2):
                    xw_steps(at, (0, 1, 2))

                def a_max(t):
                    if at.live(2):
                        wait(dve, exps_ready, at.tile(2, t))
                        dve.tensor_tensor(alpha[:, t, :], alpha[:, t, :], e2[:, t % 2, :], ALU.max).then_inc(max_ready, 1)

                def a_mul(t):
                    if at.live(2):
                        wait(dve, max_ready, at.tile(2, t))
                        if t == 0:
                            wait(dve, adj_loaded[s2], at.loads(2))
                        dve.tensor_tensor(alpha[:, t, :], alpha[:, t, :], adj[:, s2, t, :],
                                          ALU.mult).then_inc(alpha_ready, 1)

                def h_sum(t):
                    if at.live(1):
                        wait(dve, ty1_done, at.tile(1, t))
                        other, k = (t - 2, 1) if t >= 2 else (t + 2, 0)
                        wait(dve, r_ready, at.tile(k, other))
                        dve.scalar_tensor_tensor(h[:, t % 2, :], TY1[t][:, 0:D], inv0[:, t:t + 1], u0[:, s1, t, 0:D],
                                                 ALU.mult, ALU.add).then_inc(h_ready, 1)

                def residual0(t):
                    if at.live(1):
                        wait(dve, h_ready, at.tile(1, t))
                        if t == 0:
                            wait(dve, x_loaded[s1], at.loads(1))
                        wait(dve, x1_ready, at.tile(0, t))
                        dve.scalar_tensor_tensor(r[:, t, :], h[:, t % 2, :], 0.0, x_sb[:, s1, t, :],
                                                 ALU.max, ALU.add).then_inc(r_ready, 1)

                def stat0(t):
                    if at.live(1):
                        wait(dve, r_ready, at.tile(1, t))
                        dve.bn_stats(stats0[:, t, :], r[:, t, :]).then_inc(stats0_ready, 1)

                def mean_var0(t):
                    if at.live(1):
                        wait(dve, stats0_ready, at.tile(1, t))
                        wait(dve, x1_ready, at.tile(0, t))
                        dve.sem_inc(passed, 1)
                        dve.bn_aggr(mv0[:, t, :], stats0[:, t, :]).then_inc(mv0_ready, 1)

                def norm0(t):
                    if at.live(1):
                        if t == 0:
                            wait(dve, x1_bv_ready, at.done(0))
                            wait(dve, x1t_done, at.done(0))
                        if t % 2 == 0:
                            wait(dve, rstd0_ready, at.chunk(1, t // 2))
                        dve.tensor_scalar(x1[:, t, :], r[:, t, :], mv0[:, t, 0:1], rstd0[:, t:t + 1],
                                          ALU.subtract, ALU.mult).then_inc(x1_ready, 1)

                def inverse1(t):
                    if at.live(0):
                        wait(dve, pv_done, at.tile(0, t))
                        dve.reciprocal(inv1[:, t:t + 1], PV[t][:, D:D + 1]).then_inc(inv1_ready, 1)

                def residual1(t):
                    if at.live(0):
                        wait(dve, inv1_ready, at.tile(0, t))
                        wait(dve, x1_bv_ready, at.tile(0, t))
                        wait(dve, out_ready, at.done(-1))
                        dve.scalar_tensor_tensor(r2[:, t, :], PV[t][:, 0:D], inv1[:, t:t + 1], x1_bv[:, t, :],
                                                 ALU.mult, ALU.add).then_inc(r2_ready, 1)

                def stat1(t):
                    if at.live(0):
                        wait(dve, r2_ready, at.tile(0, t))
                        dve.bn_stats(stats1[:, t, :], r2[:, t, :]).then_inc(stats1_ready, 1)

                def mean_var1(t):
                    if at.live(0):
                        wait(dve, stats1_ready, at.tile(0, t))
                        wait(dve, shift1_ready, at.chunk(-1, t // 2))
                        dve.sem_inc(passed, 1)
                        dve.bn_aggr(mv1[:, t, :], stats1[:, t, :]).then_inc(mv1_ready, 1)

                h_sum(0)
                residual0(0)
                h_sum(1)
                stat0(0)
                residual0(1)
                mean_var0(0)
                h_sum(2)
                stat0(1)
                residual0(2)
                mean_var0(1)
                h_sum(3)
                stat0(2)
                residual0(3)
                mean_var0(2)
                stat0(3)
                norm0(0)
                mean_var0(3)
                norm0(1)
                if at.live(2):
                    xw_steps(at, (3,))
                norm0(2)
                norm0(3)
                inverse1(0)
                residual1(0)
                stat1(0)
                if at.live(0):
                    a_max(0)
                inverse1(1)
                residual1(1)
                mean_var1(0)
                if at.live(1):
                    for c in range(C):
                        wait(dve, x1t_hi_ready, at.chunk(1, c))
                        split_lo(x1t_lo[:, c, :], X1T[c][:, :], x1t_hi[:, c, :]).then_inc(x1t_lo_ready, T // C)
                if not at.live(0):
                    a_max(0)
                inverse1(2)
                stat1(1)
                residual1(2)
                a_mul(0)
                mean_var1(1)
                stat1(2)
                a_max(1)
                inverse1(3)
                a_mul(1)
                residual1(3)
                mean_var1(2)
                stat1(3)
                a_max(2)
                a_mul(2)
                mean_var1(3)
                if at.live(1):
                    for c in range(C):
                        wait(dve, g_hi_ready, at.chunk(1, c))
                        dve.scalar_tensor_tensor(g_lo[:, c, :], G[c][:, :], g_bias[:, c:c + 1], plain(g_hi[:, c, :]),
                                                 ALU.add, ALU.subtract).then_inc(g_lo_ready, T // C)
                a_max(3)
                if at.live(1):
                    for t in range(T):
                        wait(dve, v_hi_ready, at.tile(1, t))
                        dve.tensor_tensor(gamma[:, t:t + 1], V[t][:, D:D + 1], gamma_bias[:, :], ALU.add).then_inc(gamma_ready, 1)
                        split_lo(v_lo[:, t, :], V[t][:, 0:D], v_hi[:, t, 0:D]).then_inc(v_lo_ready, 1)
                        if t == 0:
                            a_mul(3)
                else:
                    a_mul(3)

                if at.it == -2 and at.pair is None:
                    dve.wait_ge(m_done, 1)
                    dve.wait_ge(w1_loaded, 16 * 4)
                    dve.tensor_copy(g_bias[:, :], ps[2][:, 0:C]).then_inc(setup_step, 1)
                    for c in range(C):
                        dve.tensor_copy(wvt_raw[:, c, D:D + 1], ps[2][:, C + c:C + c + 1]).then_inc(setup_step, 1)
                        dve.memset(wvt_raw[:, c, D + 1:E], 0.0).then_inc(setup_step, 1)
                        dve.tensor_copy(m_hi[:, c, :], ps[c][:, 0:D]).then_inc(setup_step, 1)
                    dve.wait_ge(setup_step, layer0_steps + 1 + 3 * C)
                    dve.tensor_copy(wv_hi[:, :, :], wvt_raw).then_inc(setup_step, 1)
                    dve.scalar_tensor_tensor(dots[:, 6, :], bq_b, 1.0, bk_b, ALU.mult, ALU.mult,
                                             accum_out=gamma_bias[:, :]).then_inc(setup_step, 1)
                    for c in range(C):
                        split_lo(m_lo[:, c, :], ps[c][:, 0:D], m_hi[:, c, :]).then_inc(setup_step, 1)
                    dve.wait_ge(setup_step, layer0_steps + 1 + 3 * C + 2 + C)
                    split_lo(wv_lo[:, :, :], wvt_raw, wv_hi[:, :, :]).then_inc(m_split, 1)
                    dve.wait_ge(m_split, 1)

            steps(dve, step, -2)

        @block.gpsimd
        def _(pool):
            def hi(dst, src):
                return pool.tensor_scalar(dst, src, 1.0, 0.0, ALU.mult, ALU.add)

            pool.memset(ident[:, :], 0.0).then_inc(consts_made, 1)
            pool.memset(minus_half[:, :], -0.5).then_inc(consts_made, 1)
            pool.memset(one_zero[:, :, 0:1], 1.0)
            pool.memset(one_zero[:, :, 1:2], 0.0).then_inc(consts_made, 1)
            pool.wait_ge(consts_made, 3)
            pool.affine_select(out=ident[:, :], in_=ident[:, :], compare_op=ALU.not_equal, fill=1.0, base=0,
                               pattern=[[-1, P]], channel_multiplier=1).then_inc(consts_made, 1)

            def inverse_deviation(at, k, pair, mv, mv_ready, var, var_ready, rstd, rstd_ready, read, tile):
                a, b = 2 * pair, 2 * pair + 2
                wait(pool, mv_ready, at.tile(k, b - 1))
                wait(pool, read, at.tile(k - 1, tile))
                pool.sem_inc(passed, 1)
                pool.tensor_scalar(var[:, a:b], mv[:, a:b, 1:2].rearrange("p t o -> p (t o)"), EPS, None,
                                   ALU.add).then_inc(var_ready, T // 2)
                wait(pool, var_ready, at.chunk(k, pair))
                pool.tensor_tensor(rstd[:, a:b], var[:, a:b], minus_half[:, a:b], ALU.pow).then_inc(rstd_ready, T // 2)

            def layer0_scale(at, pair):
                inverse_deviation(at, 1, pair, mv0, mv0_ready, var0, var0_ready, rstd0, rstd0_ready, x1_ready, 2 * pair + 1)

            def layer1_scale(at, pair):
                inverse_deviation(at, -1, pair, mv1, mv1_ready, var1, var1_ready, rstd1, rstd1_ready, out_ready, T - 1)
                wait(pool, rstd1_ready, at.chunk(-1, pair))
                pool.sem_inc(passed, 1)
                for t in range(2 * pair, 2 * pair + 2):
                    last = pool.tensor_scalar(shift1[:, t:t + 1], mv1[:, t, 0:1], rstd1[:, t:t + 1], -1.0,
                                              ALU.mult, ALU.mult)
                last.then_inc(shift1_ready, T // 2)

            def xt_split(at, k):
                for c in range(C):
                    if c == 0:
                        wait(pool, xt_loaded[at.slot(k)], at.loads(k))
                        wait(pool, w0s_done, at.done(k - 1))
                        pool.sem_inc(passed, 1)
                    split = hi(xt_hi[:, c, :], xt[:, at.slot(k), c, :])
                split.then_inc(xt_hi_ready, T)
                wait(pool, xt_hi_ready, at.done(k))
                for c in range(C):
                    split = pool.tensor_tensor(xt_lo[:, c, :], xt[:, at.slot(k), c, :], plain(xt_hi[:, c, :]), ALU.subtract)
                split.then_inc(xt_lo_ready, T)

            def alpha_split(at, t):
                wait(pool, alpha_ready, at.tile(1, t))
                wait(pool, ty1_done, at.done(-1))
                pool.sem_inc(passed, 1)
                hi(alpha_hi[:, at.slot(1), t, :], alpha[:, t, :]).then_inc(alpha_hi_ready, 1)
                wait(pool, alpha_hi_ready, at.tile(1, t))
                pool.tensor_tensor(alpha_lo[:, at.slot(1), t, :], alpha[:, t, :], plain(alpha_hi[:, at.slot(1), t, :]),
                                   ALU.subtract).then_inc(alpha_lo_ready, 1)

            def step(at):
                if at.live(2) and not (at.pair is None and at.it == -2):
                    xt_split(at, 2)
                if at.live(1):
                    for t in range(T):
                        alpha_split(at, t)
                if at.live(-1):
                    layer1_scale(at, 0)
                    layer1_scale(at, 1)
                if at.live(0):
                    if at.it == 0 and at.pair is None:
                        pool.wait_ge(w1_loaded, 16 * 4)
                        pool.wait_ge(m_split, 1)
                    for t in range(T):
                        wait(pool, x1_ready, at.tile(0, t))
                        wait(pool, r2_ready, at.tile(-1, t))
                        pool.tensor_tensor(x1_bv[:, t, :], x1[:, t, :], bv1_row[:, :], ALU.add).then_inc(x1_bv_ready, 1)
                if at.live(1):
                    layer0_scale(at, 0)
                    layer0_scale(at, 1)

            steps(pool, step, -2)


def kernel(**inputs):
    import numpy as _np
    import concourse.bacc as _bacc
    from concourse import mybir as _mybir
    from concourse.bass_utils import run_bass_kernel_spmd as _run

    a = {k: _np.asarray(v) for k, v in inputs.items()}
    x, adj = a["x"], a["adj"]
    B, N, D = x.shape
    x_t = x.reshape(B, 128, N // 128, D).transpose(0, 3, 2, 1).reshape(B, D, N)
    adj_t = adj.reshape(B, 128, N // 128, N).transpose(0, 3, 2, 1).reshape(B, N, N)
    arrays = {
        "x": x, "x_t": x_t, "adj_t": adj_t,
        "w0_all": a["L0_gnn_Wk"], "wv0": a["L0_gnn_Wv"],
        "bv0": a["L0_gnn_bv"].reshape(1, -1), "aw": a["L0_gnn_aw"].reshape(1, -1),
        "ab": a["L0_gnn_ab"].reshape(1, 1), "bk0": a["L0_gnn_bk"].reshape(1, -1),
        "wq": a["L1_gnn_Wq_w"], "wk": a["L1_gnn_Wk_w"], "wv_t": a["L1_gnn_Wv_w"].T,
        "bq_row": a["L1_gnn_Wq_b"].reshape(1, -1), "bk_row": a["L1_gnn_Wk_b"].reshape(1, -1),
        "bq_col": a["L1_gnn_Wq_b"].reshape(-1, 128).T, "bk_col": a["L1_gnn_Wk_b"].reshape(-1, 128).T,
        "bv1": a["L1_gnn_Wv_b"].reshape(1, -1),
    }
    arrays = {f"in_{k}_dram": _np.ascontiguousarray(v) for k, v in arrays.items()}
    nc = _bacc.Bacc("TRN2", target_bir_lowering=False, num_devices=1)
    args = [nc.dram_tensor(k, v.shape, _mybir.dt.from_np(v.dtype), kind="ExternalInput").ap() for k, v in arrays.items()]
    args.append(nc.dram_tensor("out_dram", (B, N, D), _mybir.dt.float32, kind="ExternalOutput").ap())
    gnn_two_layer_kernel(nc, *args)
    r = _run(nc, [arrays], core_ids=[0])
    return r.results[0]["out_dram"]
```

```python
import concourse.bass as bass
from concourse import mybir
from contextlib import ExitStack




def gnn_two_layer_kernel(nc, x, x_t, adj_t, w0_all, wv0, bv0, aw, ab, bk0, wq_bq, wk, wv_t,
                         bq_row, bk_row, bk_col, bv1, out):
    f32 = mybir.dt.float32
    f32r = mybir.dt.float32r
    ALU = mybir.AluOpType
    ACT = mybir.ActivationFunctionType

    P = 128
    B, N, D = x.shape
    T = N // P
    C = D // P
    E = D + 2
    NEG_SLOPE = 0.2
    EPS = 1e-5
    FIRST_LOOPED, LAST_LOOPED = 2, B - 3
    PAIRS = (LAST_LOOPED - FIRST_LOOPED + 1) // 2
    assert (FIRST_LOOPED, N, D) == (2, 512, 256) and 2 * PAIRS == LAST_LOOPED - 1

    ctx = ExitStack()
    with ctx:
        def sb(name, shape, dt=f32):
            return ctx.enter_context(nc.sbuf_tensor(name, shape, dt))

        def sem(name, n=None):
            if n is None:
                return ctx.enter_context(nc.semaphore(name))
            return [ctx.enter_context(nc.semaphore(f"{name}_{t}")) for t in range(n)]

        def plain(ap):
            return ap.bitcast(f32)

        ident = sb("ident", [P, P])
        minus_half = sb("minus_half", [P, T])
        one_zero = sb("one_zero", [P, T, 2])
        w_hi = sb("w_hi", [P, C, 2 * D + E], f32r)
        w_lo = sb("w_lo", [P, C, 2 * D + E], f32r)
        m_hi = sb("m_hi", [P, C, D], f32r)
        m_lo = sb("m_lo", [P, C, D], f32r)
        wv_hi = sb("wv_hi", [P, C, E], f32r)
        wv_lo = sb("wv_lo", [P, C, E], f32r)
        u0_bias = sb("u0_bias", [P, E])
        bv1_row = sb("bv1_row", [P, D])
        g_bias = sb("g_bias", [P, C])
        gamma_bias = sb("gamma_bias", [P, 1])

        adj = sb("adj_sb", [P, 2, T, N])
        x_sb = sb("x_sb", [P, 2, T, D])
        xt = sb("xt", [P, 2, C, N])
        xt_hi = sb("xt_hi", [P, C, N], f32r)
        xt_lo = sb("xt_lo", [P, C, N], f32r)
        u0 = sb("u0", [P, 2, T, E])
        xw1 = sb("xw1", [P, T, D])
        y2_hi = sb("y2_hi", [P, T, E], f32r)
        y2_lo = sb("y2_lo", [P, T, D], f32r)
        sj_slope = sb("sj_slope", [P, T])
        alpha = sb("alpha", [P, T, N])
        e2 = sb("e2", [P, 2, N])
        alpha_hi = sb("alpha_hi", [P, 2, T, N], f32r)
        alpha_lo = sb("alpha_lo", [P, 2, T, N], f32r)
        y1 = sb("y1", [P, 2, D])
        y1_hi = sb("y1_hi", [P, T, D], f32r)
        y1_lo = sb("y1_lo", [P, T, D], f32r)
        sum0 = sb("sum0", [P, T])
        inv0 = sb("inv0", [P, T])
        h = sb("h", [P, 2, D])
        x1 = sb("x1", [P, T, D])
        x1_bv = sb("x1_bv", [P, T, D])
        x1t_hi = sb("x1t_hi", [P, C, N], f32r)
        x1t_lo = sb("x1t_lo", [P, C, N], f32r)
        g_hi = sb("g_hi", [P, C, N], f32r)
        g_lo = sb("g_lo", [P, C, N], f32r)
        v_hi = sb("v_hi", [P, T, E], f32r)
        v_lo = sb("v_lo", [P, T, D], f32r)
        gamma = sb("gamma", [P, T])
        p_hi = sb("p_hi", [P, T, N], f32r)
        p_lo = sb("p_lo", [P, T, N], f32r)
        inv1 = sb("inv1", [P, T])
        stats0 = sb("stats0", [P, T, 6])
        stats1 = sb("stats1", [P, T, 6])
        mv0 = sb("mv0", [P, T, 2])
        mv1 = sb("mv1", [P, T, 2])
        var0 = sb("var0", [P, T])
        var1 = sb("var1", [P, T])
        rstd0 = sb("rstd0", [P, T])
        rstd1 = sb("rstd1", [P, T])
        shift1 = sb("shift1", [P, T])
        shared = sb("shared", [P, 5 * T * D])
        r = shared[:, 0:1024].rearrange("p (t d) -> p t d", t=T)
        r2 = shared[:, 1024:2048].rearrange("p (t d) -> p t d", t=T)
        out_sb = shared[:, 2048:3072].rearrange("p (t d) -> p t d", t=T)
        p_full = shared[:, 3072:5120].rearrange("p (t n) -> p t n", t=T)
        w_raw = shared[:, 0:C * (2 * D + E)].rearrange("p (c n) -> p c n", c=C)
        staged = C * (2 * D + E)

        def stage(n):
            nonlocal staged
            staged += n
            return shared[:, staged - n:staged]
        wv0_raw = stage(C * D).rearrange("p (c n) -> p c n", c=C)
        wq_raw = stage(C * (D + 1)).rearrange("p (c n) -> p c n", c=C)
        wk_raw = stage(C * D).rearrange("p (c n) -> p c n", c=C)
        wvt_raw = stage(C * E).rearrange("p (c n) -> p c n", c=C)
        aw_row = stage(2 * D)
        bv0_row = stage(D)
        bq_b = stage(D)
        bk_b = stage(D)
        ab_col = stage(1)
        bv0_dots = stage(3)
        bk_c = stage(C)
        assert staged <= 5 * T * D
        x1_bv_flat = x1_bv[:, :, :].rearrange("p t d -> p (t d)")
        bk0_rows = x1_bv_flat[:, 0:3 * D]
        m_raw = x1_bv_flat[:, 0:C * (D + 1)].rearrange("p (c n) -> p c n", c=C)
        dots = p_hi[:, :, :].rearrange("p t n -> p (t n)").rearrange("p (s d) -> p s d", d=D)

        ps = [ctx.enter_context(nc.psum_tensor(f"bank{i}", [P, N], f32)) for i in range(8)]
        SCORES = [ps[0], ps[2], ps[7], ps[1]]
        TY2 = [ps[3], ps[4], ps[5], ps[7]]
        XW12 = [ps[6], ps[1], ps[3], ps[4]]
        XW0S = [ps[0], ps[2], ps[7], ps[5]]
        SI = ps[7]
        TY1 = [ps[6], ps[0], ps[1], ps[2]]
        PV = [ps[3], ps[6], ps[4], ps[5]]
        X1T = [ps[0], ps[1]]
        G = [ps[2], ps[3]]
        V = [ps[6], ps[4], ps[5], ps[1]]
        M = [ps[4], ps[5]]

        def ty1_bank(at, t):
            return TY2[t] if at.is_step(-1) else TY1[t]

        def xw_banks(at, t):
            n = 0 if at.is_step(-1) and t == 2 else t
            return XW12[n], XW0S[n]

        w12_loaded, w0_loaded, wa_loaded = sem("w12_loaded"), sem("w0_loaded"), sem("wa_loaded")
        wqk_loaded, w1_loaded = sem("wqk_loaded"), sem("w1_loaded")
        adj_loaded, x_loaded, xt_loaded = sem("adj_loaded", 2), sem("x_loaded", 2), sem("xt_loaded", 2)
        out_stored = sem("out_stored")
        consts_made = sem("consts_made")
        w12_hi_made, w0s_hi_made = sem("w12_hi_made"), sem("w0s_hi_made")
        w12_split, w0s_split = sem("w12_split"), sem("w0s_split")
        alpha3_hi_made, alpha3_split = sem("alpha3_hi_made"), sem("alpha3_split")
        m_done, m_copied, wk_bq_placed = sem("m_done"), sem("m_copied"), sem("wk_bq_placed")
        w1_hi_made, w1_split, setup_step = sem("w1_hi_made"), sem("w1_split"), sem("setup_step")
        ones_made = sem("ones_made")
        w12_done, w0s_done, si_done = sem("w12_done"), sem("w0s_done"), sem("si_done")
        ty2_done, ty1_done, pv_done = sem("ty2_done"), sem("ty1_done"), sem("pv_done")
        scores_done, x1t_done = sem("scores_done"), sem("x1t_done")
        g_done, v_done = sem("g_done"), sem("v_done")
        xw1_ready, y2_hi_ready, y1_hi_ready = sem("xw1_ready"), sem("y2_hi_ready"), sem("y1_hi_ready")
        exps_ready, out_ready = sem("exps_ready"), sem("out_ready")
        p_exp_ready, p_hi_ready = sem("p_exp_ready"), sem("p_hi_ready")
        x1t_hi_ready, g_hi_ready, v_hi_ready = sem("x1t_hi_ready"), sem("g_hi_ready"), sem("v_hi_ready")
        u0_ready, y2_lo_ready, sj_slope_ready = sem("u0_ready"), sem("y2_lo_ready"), sem("sj_slope_ready")
        sum0_ready, inv0_ready = sem("sum0_ready"), sem("inv0_ready")
        y1_ready, y1_lo_ready = sem("y1_ready"), sem("y1_lo_ready")
        max_ready, alpha_ready = sem("max_ready"), sem("alpha_ready")
        p_ready, p_lo_ready = sem("p_ready"), sem("p_lo_ready")
        h_ready, r_ready, x1_ready = sem("h_ready"), sem("r_ready"), sem("x1_ready")
        stats0_ready, mv0_ready = sem("stats0_ready"), sem("mv0_ready")
        inv1_ready, r2_ready, stats1_ready, mv1_ready = sem("inv1_ready"), sem("r2_ready"), sem("stats1_ready"), sem("mv1_ready")
        x1t_lo_ready, g_lo_ready, v_lo_ready = sem("x1t_lo_ready"), sem("g_lo_ready"), sem("v_lo_ready")
        gamma_ready = sem("gamma_ready")
        xt_hi_ready, xt_lo_ready = sem("xt_hi_ready"), sem("xt_lo_ready")
        alpha_hi_ready, alpha_lo_ready = sem("alpha_hi_ready"), sem("alpha_lo_ready")
        var0_ready, rstd0_ready = sem("var0_ready"), sem("rstd0_ready")
        var1_ready, rstd1_ready, shift1_ready = sem("var1_ready"), sem("rstd1_ready"), sem("shift1_ready")
        x1_bv_ready = sem("x1_bv_ready")
        passed = sem("passed")

        block = ctx.enter_context(nc.Block())

        class Step:
            def __init__(self, eng, pair, it, values):
                self.eng, self.pair, self.it, self.values = eng, pair, it, values

            def value(self, key, make):
                if key not in self.values:
                    self.values[key] = self.eng.snap(make())
                return self.values[key]

            def tile(self, k, t):
                n = T * (self.it + k) + t + 1
                if self.pair is None:
                    return n
                return self.value(n, lambda: self.pair * (2 * T) + n)

            def chunk(self, k, c):
                return self.tile(k, (c + 1) * (T // 2) - 1)

            def done(self, k):
                return self.tile(k, T - 1)

            def loads(self, k):
                n = 16 * ((self.it + k) // 2 + 1)
                if self.pair is None:
                    return n
                return self.value(("loads", n), lambda: self.pair * 16 + n)

            def stores(self, k):
                n = 16 * (self.it + k + 1)
                if self.pair is None:
                    return n
                return self.value(("stores", n), lambda: self.pair * 32 + n)

            def live(self, k):
                return self.pair is not None or 0 <= self.it + k < B

            def is_step(self, it):
                return self.pair is None and self.it == it

            def slot(self, k):
                return (self.it + k) % 2

            def graph(self, k):
                return self.it + k if self.pair is None else self.pair * 2 + (self.it + k)

        def steps(eng, step, first):
            for it in range(first, FIRST_LOOPED):
                step(Step(eng, None, it, {}))
            with eng.Fori(1, PAIRS + 1) as pair:
                values = {}
                step(Step(eng, pair, 0, values))
                step(Step(eng, pair, 1, values))
            for it in range(LAST_LOOPED + 1, B + 1):
                step(Step(eng, None, it, {}))

        def wait(eng, semaphore, count):
            if not isinstance(count, int) or count > 0:
                eng.wait_ge(semaphore, count)

        @block.sync
        def _(sp):
            def load(dst, src, semaphore):
                sp.dma_start(dst, src).then_inc(semaphore, 16)

            def load_xt(slot, graph):
                load(xt[:, slot, :, :], x_t[graph].rearrange("(p c) n -> p c n", c=C), xt_loaded[slot])

            def load_x(slot, graph):
                load(x_sb[:, slot, :, :], x[graph].rearrange("(p t) d -> p t d", t=T), x_loaded[slot])

            def load_adj(slot, graph):
                load(adj[:, slot, :, :], adj_t[graph].rearrange("(p t) n -> p t n", t=T), adj_loaded[slot])

            load_xt(0, 0)
            load(w_raw[:, :, 0:D], w0_all[1].rearrange("(p c) n -> p c n", c=C), w12_loaded)
            load(w_raw[:, :, D:2 * D], w0_all[2].rearrange("(p c) n -> p c n", c=C), w12_loaded)
            load(wv0_raw, wv0.rearrange("(p c) n -> p c n", c=C), wa_loaded)
            load(aw_row, aw.to_broadcast([P, 2 * D]), wa_loaded)
            load(bv0_row, bv0.to_broadcast([P, D]), wa_loaded)
            load(ab_col, ab.to_broadcast([P, 1]), wa_loaded)
            load(w_raw[:, :, 2 * D:3 * D], w0_all[0].rearrange("(p c) n -> p c n", c=C), w0_loaded)
            load(bk0_rows, bk0.to_broadcast([P, 3 * D]), w0_loaded)
            load_xt(1, 1)
            load(wq_raw, wq_bq.rearrange("(c p) n -> p c n", p=P), wqk_loaded)
            load(wk_raw, wk.rearrange("(c p) n -> p c n", p=P), wqk_loaded)
            load(bk_c, bk_col, wqk_loaded)
            load_adj(0, 0)
            load(wvt_raw[:, :, 0:D], wv_t.rearrange("(c p) n -> p c n", p=P), w1_loaded)
            load(bq_b, bq_row.to_broadcast([P, D]), w1_loaded)
            load(bk_b, bk_row.to_broadcast([P, D]), w1_loaded)
            load(bv1_row[:, :], bv1.to_broadcast([P, D]), w1_loaded)
            load_x(0, 0)
            load_adj(1, 1)
            load_x(1, 1)

            def step(at):
                if at.live(0) and at.live(2):
                    wait(sp, xt_lo_ready, at.done(0))
                    load_xt(at.slot(2), at.graph(2))
                    wait(sp, r_ready, at.tile(0, T - 1))
                    load_x(at.slot(2), at.graph(2))
                if at.is_step(B):
                    rows = out[B - 1].rearrange("(p t) d -> p t d", t=T)
                    for half in range(2):
                        some = slice(half * T // 2, (half + 1) * T // 2)
                        wait(sp, out_ready, at.chunk(-1, half))
                        sp.dma_start(rows[:, some, :], out_sb[:, some, :]).then_inc(out_stored, 16)
                elif at.live(-1):
                    wait(sp, out_ready, at.done(-1))
                    sp.dma_start(out[at.graph(-1)].rearrange("(p t) d -> p t d", t=T),
                                 out_sb).then_inc(out_stored, 16)
                if at.live(0) and at.live(2):
                    wait(sp, p_ready, at.tile(0, T - 1))
                    load_adj(at.slot(2), at.graph(2))

            steps(sp, step, 0)
            sp.wait_ge(out_stored, 16 * (B + 1))

        @block.tensor
        def _(pe):
            def product(dst, terms):
                for n, (stationary, moving) in enumerate(terms):
                    width = moving.shape[-1]
                    last = pe.matmul(dst[:, 0:width], stationary, moving,
                                     start=(n == 0), stop=(n == len(terms) - 1))
                return last

            def nodes(t):
                return slice(t * P, (t + 1) * P)

            def scores(at):
                wait(pe, g_hi_ready, at.done(0))
                for t in range(T):
                    if t == 2 and at.live(1):
                        wait(pe, exps_ready, at.done(1))
                    elif t == T - 1:
                        wait(pe, v_lo_ready, at.done(0))
                    for c in range(C):
                        pe.matmul(SCORES[t][:, :], g_hi[:, c, nodes(t)], x1t_hi[:, c, :], start=(c == 0), stop=False)
                        pe.matmul(SCORES[t][:, :], g_hi[:, c, nodes(t)], x1t_lo[:, c, :], start=False, stop=False)
                    if t == 0:
                        wait(pe, g_lo_ready, at.done(0))
                    for c in range(C):
                        last = pe.matmul(SCORES[t][:, :], g_lo[:, c, nodes(t)], x1t_hi[:, c, :],
                                         start=False, stop=(c == C - 1))
                    last.then_inc(scores_done, 1)

            def aggregate(dst, a_hi, a_lo, y_hi, y_lo, t, sources=range(T), arrive=None):
                for j in sources:
                    if arrive is not None:
                        arrive(j)
                    terms = ((a_hi, y_hi), (a_lo, y_hi), (a_hi, y_lo))
                    for n, (a, y) in enumerate(terms):
                        last = pe.matmul(dst[:, 0:y.shape[-1]], a[:, j, nodes(t)], y[:, j, :],
                                         start=(j == 0 and n == 0), stop=(j == T - 1 and n == 2))
                return last

            def ty2(at):
                def alpha_tile(j):
                    wait(pe, alpha_lo_ready, at.tile(1, j))

                wait(pe, y2_lo_ready, at.done(1))
                a_hi, a_lo = alpha_hi[:, at.slot(1), :, :], alpha_lo[:, at.slot(1), :, :]
                for t in range(T):
                    if t == T - 1:
                        if at.live(0):
                            wait(pe, p_exp_ready, at.done(0))
                        else:
                            wait(pe, exps_ready, at.done(1))
                    elif at.is_step(-1) and t == 1:
                        pe.wait_ge(m_copied, 3)
                    aggregate(TY2[t], a_hi, a_lo, y2_hi, y2_lo, t,
                              arrive=alpha_tile if t == 0 else None).then_inc(ty2_done, 1)

            def xw(at, tiles, parts=("w12", "w0s")):
                x_hi, x_lo = (x1t_hi, x1t_lo) if at.is_step(-1) else (xt_hi, xt_lo)
                if 0 in tiles:
                    wait(pe, xt_lo_ready, at.done(2))
                for t in tiles:
                    if at.is_step(-1):
                        if t == 0:
                            wait(pe, y2_lo_ready, at.tile(1, 1))
                        elif t == 2:
                            wait(pe, y2_lo_ready, at.tile(2, 0))
                        elif t == 3:
                            wait(pe, h_ready, at.tile(1, 2))
                    elif t == 2:
                        wait(pe, y1_ready, at.done(1))
                    to12, to0s = xw_banks(at, t)
                    passes = [(s[:, c, nodes(t)], w, c) for c in range(C)
                              for s, w in ((x_hi, w_hi), (x_hi, w_lo), (x_lo, w_hi))]
                    for n, (x_part, w_part, c) in enumerate(passes):
                        if at.is_step(-2) and t == 0 and n % 3 == 0:
                            if "w12" in parts:
                                pe.wait_ge(w12_split, c + 1)
                            if "w0s" in parts:
                                pe.wait_ge(w0s_split, c + 1)
                        start, stop = n == 0, n == len(passes) - 1
                        if "w12" in parts:
                            last12 = pe.matmul(to12[:, :], x_part, w_part[:, c, 0:2 * D], start=start, stop=stop)
                        if "w0s" in parts:
                            last0s = pe.matmul(to0s[:, 0:E], x_part, w_part[:, c, 2 * D:2 * D + E], start=start, stop=stop)
                    if "w12" in parts:
                        last12.then_inc(w12_done, 1)
                    if "w0s" in parts:
                        last0s.then_inc(w0s_done, 1)

            def si_rows(at):
                wait(pe, u0_ready, at.done(2))
                for t in range(T):
                    column = u0[:, at.slot(2), t, D + 1:D + 2]
                    last = pe.transpose(SI[:, nodes(t)], column.to_broadcast([P, P]), ident[:, :])
                last.then_inc(si_done, T)

            def ty1(at, t, sources=range(T)):
                def y1_tile(j):
                    wait(pe, y1_lo_ready, at.tile(1, j))

                if t in (0, 2) and at.live(2) and not at.is_step(-1):
                    wait(pe, y2_lo_ready, at.tile(2, t // 2))
                last = aggregate(ty1_bank(at, t), alpha_hi[:, at.slot(1), :, :], alpha_lo[:, at.slot(1), :, :],
                                 y1_hi, y1_lo, t, sources, y1_tile if t == 0 else None)
                if T - 1 in sources:
                    last.then_inc(ty1_done, 1)

            def ty1_as_y1_comes(at):
                for sources in ((0, 1), (2, 3)):
                    ty1(at, 0, sources)
                    ty1(at, 1, sources)
                ty1(at, 2)
                ty1(at, 3)

            def pv(at, t, sources=range(T)):
                def p_tile(j):
                    wait(pe, p_lo_ready, at.tile(0, j))

                if t == 0:
                    if at.live(2):
                        wait(pe, y2_lo_ready, at.tile(2, 2))
                    elif at.live(1):
                        wait(pe, y1_ready, at.tile(1, 0))
                elif t == 1 and at.live(1):
                    wait(pe, h_ready, at.tile(1, 0))
                elif t == 2 and at.live(2):
                    wait(pe, y2_lo_ready, at.done(2))
                last = aggregate(PV[t], p_hi, p_lo, v_hi, v_lo, t, sources, p_tile if t == 0 else None)
                if T - 1 in sources:
                    last.then_inc(pv_done, 1)

            def x1_transposes(at):
                wait(pe, h_ready, at.done(1))
                if at.is_step(-1):
                    wait(pe, y2_lo_ready, at.tile(2, 2))
                for c in range(C):
                    for t in range(T):
                        if c == 0:
                            wait(pe, x1_ready, at.tile(1, t))
                        last = pe.transpose(X1T[c][:, nodes(t)], x1[:, t, nodes(c)], ident[:, :])
                    last.then_inc(x1t_done, T // C)

            def g_product(at):
                if at.is_step(-1):
                    pe.wait_ge(w1_split, 1)
                for cc in range(C):
                    wait(pe, x1t_hi_ready, at.chunk(1, cc))
                    for c in range(C):
                        if cc == 0 and c == 1 and at.live(0):
                            wait(pe, r2_ready, at.tile(0, 0))
                        pe.matmul(G[c][:, :], m_hi[:, cc, nodes(c)], x1t_hi[:, cc, :], start=(cc == 0), stop=False)
                        pe.matmul(G[c][:, :], m_lo[:, cc, nodes(c)], x1t_hi[:, cc, :], start=False, stop=False)
                    wait(pe, x1t_lo_ready, at.chunk(1, cc))
                    for c in range(C):
                        last = pe.matmul(G[c][:, :], m_hi[:, cc, nodes(c)], x1t_lo[:, cc, :],
                                         start=False, stop=(cc == C - 1))
                        if cc == C - 1:
                            last.then_inc(g_done, T // C)

            def v_product(at):
                for t in range(T):
                    if t < T - 1:
                        if at.is_step(-1) and t == 1:
                            wait(pe, y2_lo_ready, at.done(2))
                        if at.live(0):
                            wait(pe, r2_ready, at.tile(0, t + 1))
                    product(V[t], [
                        (s[:, c, nodes(t)], m[:, c, :])
                        for c in range(C) for s, m in ((x1t_hi, wv_hi), (x1t_hi, wv_lo), (x1t_lo, wv_hi))
                    ]).then_inc(v_done, 1)

            def step(at):
                if at.is_step(-2):
                    first_step(at)
                    return
                if at.is_step(-1):
                    ahead_step(at)
                    return
                if not at.live(2):
                    closing_step(at)
                    return
                scores(at)
                ty2(at)
                xw(at, (0, 1, 2))
                for t in range(T):
                    ty1(at, t)
                xw(at, (3,))
                pv(at, 0)
                si_rows(at)
                pv(at, 1)
                x1_transposes(at)
                pv(at, 2)
                pv(at, 3)
                g_product(at)
                v_product(at)

            def first_step(at):
                xw(at, (0, 1), ("w12",))
                xw(at, range(T), ("w0s",))
                xw(at, (2,), ("w12",))
                pe.wait_ge(consts_made, 4)
                si_rows(at)
                xw(at, (3,), ("w12",))

            def layer1_weights(at):
                pe.wait_ge(wqk_loaded, 16 * 3)
                pe.wait_ge(y2_lo_ready, T)
                for c in range(C):
                    product(M[c], [(wk_raw[:, o, nodes(c)], wq_raw[:, o, :]) for o in range(C)])
                for c in range(C):
                    last = product(M[0][:, E + c:E + c + 1], [(wq_raw[:, o, nodes(c)], bk_c[:, o:o + 1]) for o in range(C)])
                last.then_inc(m_done, 1)

            def ahead_step(at):
                xw(at, (0, 1))
                layer1_weights(at)
                ty2(at)
                ty1_as_y1_comes(at)
                xw(at, (2, 3))
                x1_transposes(at)
                si_rows(at)
                g_product(at)
                v_product(at)

            def closing_step(at):
                if at.live(0):
                    scores(at)
                if at.live(1):
                    ty2(at)
                    pv(at, 0)
                    ty1_as_y1_comes(at)
                    pv(at, 1)
                    pv(at, 2)
                    pv(at, 3, (0, 1))
                    x1_transposes(at)
                    pv(at, 3, (2, 3))
                    g_product(at)
                    v_product(at)
                elif at.live(0):
                    for j in range(T):
                        for t in range(T - 1):
                            pv(at, t, (j,))
                    pv(at, T - 1)

            steps(pe, step, -2)

        @block.scalar
        def _(act):
            def step(at):
                s2 = at.slot(2)

                def exp_p(t):
                    wait(act, scores_done, at.tile(0, t))
                    wait(act, gamma_ready, at.tile(0, t))
                    wait(act, p_lo_ready, at.tile(-1, t))
                    act.activation(p_full[:, t, :], SCORES[t][:, :], ACT.Exp,
                                   bias=gamma[:, t:t + 1]).then_inc(p_exp_ready, 1)

                def hi_p(t):
                    wait(act, p_ready, at.tile(0, t))
                    if t == 0:
                        wait(act, pv_done, at.done(-1))
                    act.activation(p_hi[:, t, :], p_full[:, t, :], ACT.Copy).then_inc(p_hi_ready, 1)

                if at.live(0):
                    exp_p(0)
                    exp_p(1)
                    hi_p(0)
                    exp_p(2)
                    hi_p(1)
                    exp_p(3)
                    hi_p(2)
                    hi_p(3)
                if at.live(1):
                    for t in range(T):
                        wait(act, y1_ready, at.tile(1, t))
                        if t == 0:
                            wait(act, ty1_done, at.done(0))
                        act.activation(y1_hi[:, t, :], y1[:, t % 2, :], ACT.Copy).then_inc(y1_hi_ready, 1)

                def xw_tile(t):
                    wait(act, w12_done, at.tile(2, t))
                    if t == 0:
                        wait(act, y1_ready, at.done(1))
                    act.activation(xw1[:, t, :], xw_banks(at, t)[0][:, 0:D], ACT.Copy).then_inc(xw1_ready, 1)
                    act.activation(y2_hi[:, t, 0:D], xw_banks(at, t)[0][:, D:2 * D], ACT.Copy).then_inc(y2_hi_ready, 1)

                if at.live(2):
                    xw_tile(0)
                    xw_tile(1)
                    if not at.is_step(-2):
                        xw_tile(2)
                    if at.is_step(-1):
                        xw_tile(3)
                if at.live(-1):
                    for t in range(T // 2 if at.is_step(B) else T):
                        if t == 0:
                            wait(act, out_stored, at.stores(-2))
                        if t % 2 == 0:
                            wait(act, shift1_ready, at.chunk(-1, t // 2))
                        norm = act.activation(out_sb[:, t, :], r2[:, t, :], ACT.Identity,
                                              scale=rstd1[:, t:t + 1], bias=shift1[:, t:t + 1])
                        if t % 2 == 1:
                            norm.then_inc(out_ready, T // 2)
                if at.live(0) and at.live(2):
                    xw_tile(3)

                def g_tiles():
                    if at.is_step(-1):
                        act.wait_ge(m_copied, 3)
                    for c in range(C):
                        wait(act, g_done, at.chunk(1, c))
                        act.activation(g_hi[:, c, :], G[c][:, :], ACT.Identity,
                                       bias=g_bias[:, c:c + 1]).then_inc(g_hi_ready, T // C)

                def exps(t):
                    if at.live(2):
                        if t == 0:
                            wait(act, si_done, at.done(2))
                            wait(act, sj_slope_ready, at.done(2))
                        wait(act, alpha_lo_ready, at.tile(1, t))
                        act.activation(alpha[:, t, :], SI[:, :], ACT.Exp, bias=u0[:, s2, t, D:D + 1])
                        if t < 2:
                            wait(act, max_ready, at.tile(1, t + 2))
                        else:
                            wait(act, max_ready, at.tile(2, t - 2))
                        act.activation(e2[:, t % 2, :], SI[:, :], ACT.Exp, scale=NEG_SLOPE,
                                       bias=sj_slope[:, t:t + 1]).then_inc(exps_ready, 1)

                if at.live(0):
                    exps(0)
                if at.live(1):
                    for c in range(C):
                        wait(act, x1t_done, at.chunk(1, c))
                        if c == 0:
                            wait(act, scores_done, at.done(0))
                        act.activation(x1t_hi[:, c, :], X1T[c][:, :], ACT.Copy).then_inc(x1t_hi_ready, T // C)
                if not at.live(0):
                    exps(0)
                if at.is_step(-2):
                    xw_tile(2)
                    xw_tile(3)
                exps(1)
                exps(2)
                if at.live(1):
                    g_tiles()
                exps(3)
                if at.is_step(-2):
                    wait(act, alpha_ready, at.done(2))
                    act.activation(alpha_hi[:, s2, T - 1, :], alpha[:, T - 1, :], ACT.Copy).then_inc(alpha3_hi_made, 1)
                    act.wait_ge(m_done, 1)
                    act.activation(g_bias[:, :], M[0][:, E:E + C], ACT.Copy).then_inc(m_copied, 1)
                    for c in range(C):
                        act.activation(m_raw[:, c, :], M[c][:, 0:D + 1], ACT.Copy).then_inc(m_copied, 1)
                if at.live(1):
                    for t in range(T):
                        wait(act, v_done, at.tile(1, t))
                        if t == 0:
                            wait(act, pv_done, at.done(0))
                        act.activation(v_hi[:, t, 0:D], V[t][:, 0:D], ACT.Copy).then_inc(v_hi_ready, 1)

            act.wait_ge(ones_made, 2)
            steps(act, step, -2)

        @block.vector
        def _(dve):
            def split_lo(dst, src, hi):
                return dve.tensor_tensor(dst, src, plain(hi), ALU.subtract)

            dve.wait_ge(xt_loaded[0], 16)
            dve.tensor_copy(xt_hi[:, :, :], xt[:, 0, :, :]).then_inc(xt_hi_ready, T)
            dve.wait_ge(xt_hi_ready, T)
            split_lo(xt_lo[:, :, :], xt[:, 0, :, :], xt_hi[:, :, :]).then_inc(xt_lo_ready, T)
            dve.wait_ge(w12_loaded, 16 * 2)
            w12, w0s = slice(0, 2 * D), slice(2 * D, 2 * D + E)
            for c in range(C):
                dve.tensor_copy(w_hi[:, c, w12], w_raw[:, c, w12]).then_inc(w12_hi_made, 1)
                dve.wait_ge(w12_hi_made, c + 1)
                split_lo(w_lo[:, c, w12], w_raw[:, c, w12], w_hi[:, c, w12]).then_inc(w12_split, 1)
            dve.wait_ge(wa_loaded, 16 * 4)
            wanted = [(w_raw[:, c, 3 * D + half:3 * D + half + 1], wv0_raw[:, c, :], half) for c in range(C) for half in range(2)]
            wanted += [(bv0_dots[:, half:half + 1], bv0_row, half) for half in range(2)]
            for n, (dst, row, half) in enumerate(wanted):
                dve.scalar_tensor_tensor(dots[:, n, :], row, 1.0, aw_row[:, half * D:(half + 1) * D],
                                         ALU.mult, ALU.mult, accum_out=dst).then_inc(setup_step, 1)
            dve.wait_ge(w0_loaded, 16 * 2)
            dve.wait_ge(setup_step, len(wanted))
            dve.tensor_copy(w_hi[:, :, w0s], w_raw[:, :, w0s]).then_inc(w0s_hi_made, 1)
            dve.wait_ge(w0s_hi_made, 1)
            split_lo(w_lo[:, :, w0s], w_raw[:, :, w0s], w_hi[:, :, w0s]).then_inc(w0s_split, C)
            dve.tensor_tensor(u0_bias[:, 0:D], bk0_rows[:, 0:D], bk0_rows[:, D:2 * D], ALU.add).then_inc(setup_step, 1)
            dve.memset(u0_bias[:, D:E], 0.0).then_inc(setup_step, 1)
            dve.tensor_tensor(bv0_dots[:, 2:3], bv0_dots[:, 0:1], bv0_dots[:, 1:2], ALU.add).then_inc(setup_step, 1)
            dve.wait_ge(setup_step, len(wanted) + 3)
            dve.tensor_tensor(u0_bias[:, D:D + 1], bv0_dots[:, 2:3], ab_col, ALU.add).then_inc(setup_step, 1)
            dve.tensor_tensor(u0_bias[:, 0:D], u0_bias[:, 0:D], bk0_rows[:, 2 * D:3 * D], ALU.add).then_inc(setup_step, 1)
            layer0_steps = len(wanted) + 5
            dve.wait_ge(setup_step, layer0_steps)
            dve.wait_ge(consts_made, 4)
            dve.tensor_copy(y2_hi[:, :, D:E], one_zero[:, :, :]).then_inc(ones_made, 1)
            dve.tensor_copy(v_hi[:, :, D:E], one_zero[:, :, :]).then_inc(ones_made, 1)

            def u0_tile(at, t):
                wait(dve, w0s_done, at.tile(2, t))
                dve.tensor_tensor(u0[:, at.slot(2), t, :], xw_banks(at, t)[1][:, 0:E], u0_bias[:, :],
                                  ALU.add).then_inc(u0_ready, 1)

            def y2_lo_tile(at, t):
                wait(dve, y2_hi_ready, at.tile(2, t))
                split_lo(y2_lo[:, t, :], xw_banks(at, t)[0][:, D:2 * D], y2_hi[:, t, 0:D]).then_inc(y2_lo_ready, 1)

            def sj_slopes(at):
                wait(dve, u0_ready, at.done(2))
                wait(dve, exps_ready, at.done(1))
                dve.tensor_scalar(sj_slope[:, :], u0[:, at.slot(2), :, D:D + 1].rearrange("p t o -> p (t o)"),
                                  NEG_SLOPE, None, ALU.mult).then_inc(sj_slope_ready, T)

            def xw_steps(at, tiles):
                for t in tiles:
                    u0_tile(at, t)
                    y2_lo_tile(at, t)
                if T - 1 in tiles:
                    sj_slopes(at)

            def step(at):
                s0, s1, s2 = at.slot(0), at.slot(1), at.slot(2)

                def p_mul(t):
                    if at.live(0):
                        wait(dve, p_exp_ready, at.tile(0, t))
                        dve.tensor_tensor(p_full[:, t, :], p_full[:, t, :], adj[:, s0, t, :],
                                          ALU.mult).then_inc(p_ready, 1)

                def p_split(t):
                    if at.live(0):
                        wait(dve, p_hi_ready, at.tile(0, t))
                        split_lo(p_lo[:, t, :], p_full[:, t, :], p_hi[:, t, :]).then_inc(p_lo_ready, 1)

                def y1_sum(t):
                    wait(dve, ty2_done, at.tile(1, t))
                    dve.tensor_scalar(sum0[:, t:t + 1], TY2[t][:, D:D + 1], 1e-12, None, ALU.add).then_inc(sum0_ready, 1)

                def y1_inv(t):
                    wait(dve, sum0_ready, at.tile(1, t))
                    dve.reciprocal(inv0[:, t:t + 1], sum0[:, t:t + 1]).then_inc(inv0_ready, 1)

                def y1_full(t):
                    wait(dve, inv0_ready, at.tile(1, t))
                    wait(dve, xw1_ready, at.tile(1, t))
                    other, k = (t - 2, 1) if t >= 2 else (t + 2, 0)
                    wait(dve, y1_lo_ready, at.tile(k, other))
                    dve.scalar_tensor_tensor(y1[:, t % 2, :], TY2[t][:, 0:D], inv0[:, t:t + 1], xw1[:, t, :],
                                             ALU.mult, ALU.add).then_inc(y1_ready, 1)

                def y1_split(t):
                    wait(dve, y1_hi_ready, at.tile(1, t))
                    split_lo(y1_lo[:, t, :], y1[:, t % 2, :], y1_hi[:, t, :]).then_inc(y1_lo_ready, 1)

                def y1_tile(t):
                    if at.live(1):
                        y1_sum(t)
                        y1_inv(t)
                        y1_full(t)

                p_mul(0)
                p_mul(1)
                p_split(0)
                p_mul(2)
                p_split(1)
                p_mul(3)
                p_split(2)
                y1_tile(0)
                p_split(3)
                y1_tile(1)
                if at.live(1):
                    y1_split(0)
                y1_tile(2)
                if at.live(1):
                    y1_split(1)
                y1_tile(3)
                if at.live(1):
                    y1_split(2)
                    y1_split(3)
                if at.is_step(-2):
                    y2_lo_tile(at, 0)
                    y2_lo_tile(at, 1)
                    for t in range(T):
                        u0_tile(at, t)
                    sj_slopes(at)
                elif at.live(2):
                    xw_steps(at, (0, 1) if at.is_step(-1) else (0, 1, 2))

                def a_max(t):
                    if at.live(2):
                        wait(dve, exps_ready, at.tile(2, t))
                        dve.tensor_tensor(alpha[:, t, :], alpha[:, t, :], e2[:, t % 2, :], ALU.max).then_inc(max_ready, 1)

                def a_mul(t):
                    if at.live(2):
                        wait(dve, max_ready, at.tile(2, t))
                        if t == 0:
                            wait(dve, adj_loaded[s2], at.loads(2))
                        dve.tensor_tensor(alpha[:, t, :], alpha[:, t, :], adj[:, s2, t, :],
                                          ALU.mult).then_inc(alpha_ready, 1)

                def h_sum(t):
                    if at.live(1):
                        wait(dve, ty1_done, at.tile(1, t))
                        other, k = (t - 2, 1) if t >= 2 else (t + 2, 0)
                        wait(dve, r_ready, at.tile(k, other))
                        dve.scalar_tensor_tensor(h[:, t % 2, :], ty1_bank(at, t)[:, 0:D], inv0[:, t:t + 1], u0[:, s1, t, 0:D],
                                                 ALU.mult, ALU.add).then_inc(h_ready, 1)

                def residual0(t):
                    if at.live(1):
                        wait(dve, h_ready, at.tile(1, t))
                        if t == 0:
                            wait(dve, x_loaded[s1], at.loads(1))
                        wait(dve, x1_ready, at.tile(0, t))
                        dve.scalar_tensor_tensor(r[:, t, :], h[:, t % 2, :], 0.0, x_sb[:, s1, t, :],
                                                 ALU.max, ALU.add).then_inc(r_ready, 1)

                def stat0(t):
                    if at.live(1):
                        wait(dve, r_ready, at.tile(1, t))
                        dve.bn_stats(stats0[:, t, :], r[:, t, :]).then_inc(stats0_ready, 1)

                def mean_var0(t):
                    if at.live(1):
                        wait(dve, stats0_ready, at.tile(1, t))
                        wait(dve, x1_ready, at.tile(0, t))
                        dve.sem_inc(passed, 1)
                        dve.bn_aggr(mv0[:, t, :], stats0[:, t, :]).then_inc(mv0_ready, 1)

                def norm0(t):
                    if at.live(1):
                        if t == 0:
                            wait(dve, x1_bv_ready, at.done(0))
                            wait(dve, x1t_done, at.done(0))
                        if t % 2 == 0:
                            wait(dve, rstd0_ready, at.chunk(1, t // 2))
                        dve.tensor_scalar(x1[:, t, :], r[:, t, :], mv0[:, t, 0:1], rstd0[:, t:t + 1],
                                          ALU.subtract, ALU.mult).then_inc(x1_ready, 1)

                def inverse1(t):
                    if at.live(0):
                        wait(dve, pv_done, at.tile(0, t))
                        dve.reciprocal(inv1[:, t:t + 1], PV[t][:, D:D + 1]).then_inc(inv1_ready, 1)

                def residual1(t):
                    if at.live(0):
                        wait(dve, inv1_ready, at.tile(0, t))
                        wait(dve, x1_bv_ready, at.tile(0, t))
                        wait(dve, out_ready, at.chunk(-1, t // 2))
                        dve.scalar_tensor_tensor(r2[:, t, :], PV[t][:, 0:D], inv1[:, t:t + 1], x1_bv[:, t, :],
                                                 ALU.mult, ALU.add).then_inc(r2_ready, 1)

                def stat1(t):
                    if at.live(0):
                        wait(dve, r2_ready, at.tile(0, t))
                        dve.bn_stats(stats1[:, t, :], r2[:, t, :]).then_inc(stats1_ready, 1)

                def mean_var1(t):
                    if at.live(0):
                        wait(dve, stats1_ready, at.tile(0, t))
                        wait(dve, shift1_ready, at.chunk(-1, t // 2))
                        dve.sem_inc(passed, 1)
                        dve.bn_aggr(mv1[:, t, :], stats1[:, t, :]).then_inc(mv1_ready, 1)

                h_sum(0)
                residual0(0)
                h_sum(1)
                stat0(0)
                residual0(1)
                mean_var0(0)
                h_sum(2)
                stat0(1)
                residual0(2)
                mean_var0(1)
                h_sum(3)
                stat0(2)
                residual0(3)
                mean_var0(2)
                stat0(3)
                if at.is_step(-1):
                    mean_var0(3)
                    norm0(0)
                    norm0(1)
                    xw_steps(at, (2,))
                    norm0(2)
                    norm0(3)
                    xw_steps(at, (3,))
                else:
                    norm0(0)
                    mean_var0(3)
                    norm0(1)
                    if at.live(0) and at.live(2):
                        xw_steps(at, (3,))
                    norm0(2)
                    norm0(3)
                inverse1(0)
                residual1(0)
                stat1(0)
                if at.live(0):
                    a_max(0)
                inverse1(1)
                residual1(1)
                mean_var1(0)
                if at.live(1):
                    for c in range(C):
                        wait(dve, x1t_hi_ready, at.chunk(1, c))
                        split_lo(x1t_lo[:, c, :], X1T[c][:, :], x1t_hi[:, c, :]).then_inc(x1t_lo_ready, T // C)
                if not at.live(0):
                    a_max(0)
                inverse1(2)
                stat1(1)
                residual1(2)
                a_mul(0)
                if at.is_step(-2):
                    y2_lo_tile(at, 2)
                    y2_lo_tile(at, 3)
                mean_var1(1)
                stat1(2)
                a_max(1)
                inverse1(3)
                a_mul(1)
                residual1(3)
                mean_var1(2)
                stat1(3)
                a_max(2)
                if at.live(1):
                    for c in range(C):
                        wait(dve, g_hi_ready, at.chunk(1, c))
                        dve.scalar_tensor_tensor(g_lo[:, c, :], G[c][:, :], g_bias[:, c:c + 1], plain(g_hi[:, c, :]),
                                                 ALU.add, ALU.subtract).then_inc(g_lo_ready, T // C)
                a_mul(2)
                mean_var1(3)
                a_max(3)
                if at.live(1):
                    for t in range(T):
                        wait(dve, v_hi_ready, at.tile(1, t))
                        dve.tensor_tensor(gamma[:, t:t + 1], V[t][:, D:D + 1], gamma_bias[:, :], ALU.add).then_inc(gamma_ready, 1)
                        split_lo(v_lo[:, t, :], V[t][:, 0:D], v_hi[:, t, 0:D]).then_inc(v_lo_ready, 1)
                        if t == 0:
                            a_mul(3)
                else:
                    a_mul(3)

                if at.is_step(-2):
                    dve.wait_ge(w1_loaded, 16 * 4)
                    dve.scalar_tensor_tensor(dots[:, 6, :], bq_b, 1.0, bk_b, ALU.mult, ALU.mult,
                                             accum_out=gamma_bias[:, :]).then_inc(setup_step, 1)
                    dve.wait_ge(setup_step, layer0_steps + 1)
                    dve.wait_ge(alpha3_hi_made, 1)
                    split_lo(alpha_lo[:, s2, T - 1, :], alpha[:, T - 1, :], alpha_hi[:, s2, T - 1, :]).then_inc(alpha3_split, 1)
                if at.is_step(B):
                    wait(dve, out_ready, at.chunk(-1, 0))
                    wait(dve, rstd1_ready, at.chunk(-1, 1))
                    for t in range(T // 2, T):
                        norm = dve.tensor_scalar(out_sb[:, t, :], r2[:, t, :], mv1[:, t, 0:1], rstd1[:, t:t + 1],
                                                 ALU.subtract, ALU.mult)
                    norm.then_inc(out_ready, T // 2)

            steps(dve, step, -2)

        @block.gpsimd
        def _(pool):
            def hi(dst, src):
                return pool.tensor_scalar(dst, src, 1.0, 0.0, ALU.mult, ALU.add)

            pool.memset(ident[:, :], 0.0).then_inc(consts_made, 1)
            pool.memset(minus_half[:, :], -0.5).then_inc(consts_made, 1)
            pool.memset(wvt_raw[:, :, D + 1:E], 0.0)
            pool.memset(one_zero[:, :, 0:1], 1.0)
            pool.memset(one_zero[:, :, 1:2], 0.0).then_inc(consts_made, 1)
            pool.wait_ge(consts_made, 3)
            pool.affine_select(out=ident[:, :], in_=ident[:, :], compare_op=ALU.not_equal, fill=1.0, base=0,
                               pattern=[[-1, P]], channel_multiplier=1).then_inc(consts_made, 1)

            def inverse_deviation(at, k, pair, mv, mv_ready, var, var_ready, rstd, rstd_ready, read, tile):
                a, b = 2 * pair, 2 * pair + 2
                wait(pool, mv_ready, at.tile(k, b - 1))
                wait(pool, read, at.tile(k - 1, tile))
                pool.sem_inc(passed, 1)
                pool.tensor_scalar(var[:, a:b], mv[:, a:b, 1:2].rearrange("p t o -> p (t o)"), EPS, None,
                                   ALU.add).then_inc(var_ready, T // 2)
                wait(pool, var_ready, at.chunk(k, pair))
                pool.tensor_tensor(rstd[:, a:b], var[:, a:b], minus_half[:, a:b], ALU.pow).then_inc(rstd_ready, T // 2)

            def layer0_scale(at, pair):
                inverse_deviation(at, 1, pair, mv0, mv0_ready, var0, var0_ready, rstd0, rstd0_ready, x1_ready, 2 * pair + 1)

            def layer1_scale(at, pair):
                inverse_deviation(at, -1, pair, mv1, mv1_ready, var1, var1_ready, rstd1, rstd1_ready, out_ready, T - 1)
                if at.is_step(B) and pair == 1:
                    return
                wait(pool, rstd1_ready, at.chunk(-1, pair))
                pool.sem_inc(passed, 1)
                for t in range(2 * pair, 2 * pair + 2):
                    last = pool.tensor_scalar(shift1[:, t:t + 1], mv1[:, t, 0:1], rstd1[:, t:t + 1], -1.0,
                                              ALU.mult, ALU.mult)
                last.then_inc(shift1_ready, T // 2)

            def xt_split(at):
                x_hi, x_lo = (x1t_hi, x1t_lo) if at.is_step(-1) else (xt_hi, xt_lo)
                wait(pool, xt_loaded[at.slot(2)], at.loads(2))
                if at.is_step(-1):
                    wait(pool, xt_lo_ready, at.done(1))
                else:
                    wait(pool, w0s_done, at.done(1))
                pool.sem_inc(passed, 1)
                for c in range(C):
                    split = hi(x_hi[:, c, :], xt[:, at.slot(2), c, :])
                split.then_inc(xt_hi_ready, T)
                wait(pool, xt_hi_ready, at.done(2))
                for c in range(C):
                    split = pool.tensor_tensor(x_lo[:, c, :], xt[:, at.slot(2), c, :], plain(x_hi[:, c, :]), ALU.subtract)
                split.then_inc(xt_lo_ready, T)

            def weights1_split():
                pool.wait_ge(m_copied, 3)
                pool.wait_ge(w1_loaded, 16 * 4)
                pool.sem_inc(passed, 1)
                hi(wvt_raw[:, :, D:D + 1], m_raw[:, :, D:D + 1]).then_inc(wk_bq_placed, 1)
                hi(m_hi[:, :, :], m_raw[:, :, 0:D])
                pool.wait_ge(wk_bq_placed, 1)
                pool.sem_inc(passed, 1)
                hi(wv_hi[:, :, :], wvt_raw).then_inc(w1_hi_made, 1)
                pool.wait_ge(w1_hi_made, 1)
                pool.tensor_tensor(m_lo[:, :, :], m_raw[:, :, 0:D], plain(m_hi[:, :, :]), ALU.subtract)
                pool.tensor_tensor(wv_lo[:, :, :], wvt_raw, plain(wv_hi[:, :, :]), ALU.subtract).then_inc(w1_split, 1)

            def alpha_split(at, t):
                wait(pool, alpha_ready, at.tile(1, t))
                wait(pool, ty1_done, at.done(-1))
                pool.sem_inc(passed, 1)
                hi(alpha_hi[:, at.slot(1), t, :], alpha[:, t, :]).then_inc(alpha_hi_ready, 1)
                wait(pool, alpha_hi_ready, at.tile(1, t))
                pool.tensor_tensor(alpha_lo[:, at.slot(1), t, :], alpha[:, t, :], plain(alpha_hi[:, at.slot(1), t, :]),
                                   ALU.subtract).then_inc(alpha_lo_ready, 1)

            def step(at):
                if at.live(2) and not (at.pair is None and at.it == -2):
                    xt_split(at)
                if at.live(1):
                    for t in range(T - 1):
                        alpha_split(at, t)
                    if at.is_step(-1):
                        pool.wait_ge(alpha3_split, 1)
                        wait(pool, alpha_lo_ready, at.tile(1, T - 2))
                        pool.sem_inc(alpha_hi_ready, 1)
                        pool.sem_inc(alpha_lo_ready, 1)
                    else:
                        alpha_split(at, T - 1)
                if at.is_step(-1):
                    weights1_split()
                if at.live(-1):
                    layer1_scale(at, 0)
                    layer1_scale(at, 1)
                if at.live(0):
                    if at.is_step(0):
                        pool.wait_ge(w1_split, 1)
                    for t in range(T):
                        wait(pool, x1_ready, at.tile(0, t))
                        wait(pool, r2_ready, at.tile(-1, t))
                        pool.tensor_tensor(x1_bv[:, t, :], x1[:, t, :], bv1_row[:, :], ALU.add).then_inc(x1_bv_ready, 1)
                if at.live(1):
                    layer0_scale(at, 0)
                    layer0_scale(at, 1)

            steps(pool, step, -2)


def kernel(**inputs):
    import numpy as _np
    import concourse.bacc as _bacc
    from concourse import mybir as _mybir
    from concourse.bass_utils import run_bass_kernel_spmd as _run

    a = {k: _np.asarray(v) for k, v in inputs.items()}
    x, adj = a["x"], a["adj"]
    B, N, D = x.shape
    x_t = x.reshape(B, 128, N // 128, D).transpose(0, 3, 2, 1).reshape(B, D, N)
    adj_t = adj.reshape(B, 128, N // 128, N).transpose(0, 3, 2, 1).reshape(B, N, N)
    arrays = {
        "x": x, "x_t": x_t, "adj_t": adj_t,
        "w0_all": a["L0_gnn_Wk"], "wv0": a["L0_gnn_Wv"],
        "bv0": a["L0_gnn_bv"].reshape(1, -1), "aw": a["L0_gnn_aw"].reshape(1, -1),
        "ab": a["L0_gnn_ab"].reshape(1, 1), "bk0": a["L0_gnn_bk"].reshape(1, -1),
        "wq_bq": _np.concatenate([a["L1_gnn_Wq_w"], a["L1_gnn_Wq_b"].reshape(-1, 1)], axis=1), "wk": a["L1_gnn_Wk_w"], "wv_t": a["L1_gnn_Wv_w"].T,
        "bq_row": a["L1_gnn_Wq_b"].reshape(1, -1), "bk_row": a["L1_gnn_Wk_b"].reshape(1, -1),
        "bk_col": a["L1_gnn_Wk_b"].reshape(-1, 128).T,
        "bv1": a["L1_gnn_Wv_b"].reshape(1, -1),
    }
    arrays = {f"in_{k}_dram": _np.ascontiguousarray(v) for k, v in arrays.items()}
    nc = _bacc.Bacc("TRN2", target_bir_lowering=False, num_devices=1)
    args = [nc.dram_tensor(k, v.shape, _mybir.dt.from_np(v.dtype), kind="ExternalInput").ap() for k, v in arrays.items()]
    args.append(nc.dram_tensor("out_dram", (B, N, D), _mybir.dt.float32, kind="ExternalOutput").ap())
    gnn_two_layer_kernel(nc, *args)
    r = _run(nc, [arrays], core_ids=[0])
    return r.results[0]["out_dram"]
```
